# Optimizing a Trainium2 kernel written in Bass

```python
import numpy as np
import jax
import jax.numpy as jnp

def _softmax(x, axis=-1):
    return jax.nn.softmax(x, axis=axis)

def _gelu(x):
    return jax.nn.gelu(x, approximate=True)

def _silu(x):
    return jax.nn.silu(x)

def _sigmoid(x):
    return jax.nn.sigmoid(x)

def _layernorm(x, axis=-1, eps=1e-05):
    m = jnp.mean(x, axis=axis, keepdims=True)
    v = jnp.var(x, axis=axis, keepdims=True)
    return (x - m) / jnp.sqrt(v + eps)

def _scatter_add(tgt, idx, src, axis=0):
    return tgt.at[idx].add(src)

def _segment_sum(src, seg, n):
    return jax.ops.segment_sum(src, seg, n)
kernel_name = 'mk_flamingo_gated_d1_seqx_r8_8587a5'

def setup_inputs(seed: int=0):
    np.random.seed(seed)
    _w = jnp.asarray

    def _rec_inputs():
        import jax
        import jax.numpy as jnp
        _rk = jax.random.key(seed)
        x = 0.0002417 + 0.9998 * jax.random.normal(jax.random.fold_in(_rk, 1), (16, 256, 128), jnp.float32)
        _lenS = 256 - jax.random.randint(jax.random.fold_in(_rk, 7), (16,), 0, max(1, 256 // 4) + 1, jnp.int32)
        _lenS2 = 1601 - jax.random.randint(jax.random.fold_in(_rk, 8), (16,), 0, max(1, 1601 // 4) + 1, jnp.int32)
        _ctx_1024P = jax.random.normal(jax.random.fold_in(_rk, 11), (16, 16, 128), jnp.float32)
        _ctx_1024c = jax.random.dirichlet(jax.random.fold_in(_rk, 511), 0.3 * jnp.ones((16,), jnp.float32), (16, 1601))
        _ctx_1024t = jnp.einsum('bsk,bkd->bsd', _ctx_1024c, _ctx_1024P)
        _ctx_1024t = _ctx_1024t * jax.lax.rsqrt(jnp.mean(jnp.square(_ctx_1024t)) + 1e-12) * 0.953939
        ctx_1024 = 7.22013e-05 + 1.00017 * (_ctx_1024t + 0.3 * jax.random.normal(jax.random.fold_in(_rk, 611), (16, 1601, 128), jnp.float32))
        _g = jax.random.normal(jax.random.fold_in(_rk, 9001), (2, 1), jnp.float32)
        _g = jnp.sign(_g) * jnp.maximum(jnp.abs(_g), 1.0) + (_g == 0) * 1.0
        g_xattn = _g[0]
        g_ffn = _g[1]
        return (x, ctx_1024, g_xattn, g_ffn)
    x, ctx_1024, g_xattn, g_ffn = _rec_inputs()

    def _L0_xattn_setup():
        import jax, jax.numpy as jnp
        import numpy as np
        D_MODEL = 128
        B, S = (4, 256)
        key = jax.random.key(seed)
        ks = jax.random.split(key, 10)
        s = 1.0 / np.sqrt(D_MODEL)
        return {'k': jax.random.normal(ks[0], (B, S, D_MODEL), jnp.float32), 'v': jax.random.normal(ks[1], (B, S, D_MODEL), jnp.float32), 'q': jax.random.normal(ks[2], (B, S, D_MODEL), jnp.float32), 'Wk': jax.random.normal(ks[3], (D_MODEL, D_MODEL), jnp.float32) * s, 'Wv': jax.random.normal(ks[4], (D_MODEL, D_MODEL), jnp.float32) * s, 'bv': jnp.zeros((D_MODEL,), jnp.float32), 'Wq': jax.random.normal(ks[5], (D_MODEL, D_MODEL), jnp.float32) * s, 'bq': jnp.zeros((D_MODEL,), jnp.float32), 'Wo': jax.random.normal(ks[6], (D_MODEL, D_MODEL), jnp.float32) * s, 'bo': jnp.zeros((D_MODEL,), jnp.float32)}
    _L0_xattn_all = _L0_xattn_setup()
    _L0_xattn_in = {k: v for k, v in _L0_xattn_all.items() if k in ('Wk', 'Wv', 'bv', 'Wq', 'bq', 'Wo', 'bo')}
    del _L0_xattn_all

    def _L0_ffn_setup():
        import jax, jax.numpy as jnp
        import numpy as np
        S, B, D, FF, E = (128, 2, 128, 256, 8)
        key = jax.random.key(seed)
        ks = jax.random.split(key, 8)
        s = 0.02
        return {'hidden_states': jax.random.normal(ks[0], (S, B, D), dtype=jnp.float32), 'router_w': jax.random.normal(ks[1], (E, D), dtype=jnp.float32) * s, 'expert_gate': jax.random.normal(ks[2], (E, D, FF), dtype=jnp.float32) * s, 'expert_up': jax.random.normal(ks[3], (E, D, FF), dtype=jnp.float32) * s, 'expert_down': jax.random.normal(ks[4], (E, FF, D), dtype=jnp.float32) * s, 'shared_gate': jax.random.normal(ks[5], (D, FF), dtype=jnp.float32) * s, 'shared_up': jax.random.normal(ks[6], (D, FF), dtype=jnp.float32) * s, 'shared_down': jax.random.normal(ks[7], (FF, D), dtype=jnp.float32) * s}
    _L0_ffn_all = _L0_ffn_setup()
    _L0_ffn_in = {k: v for k, v in _L0_ffn_all.items() if k in ('router_w', 'expert_gate', 'expert_up', 'expert_down', 'shared_gate', 'shared_up', 'shared_down')}
    del _L0_ffn_all
    return {'x': x, 'ctx_1024': ctx_1024, 'g_xattn': g_xattn, 'g_ffn': g_ffn, 'L0_xattn_Wk': _L0_xattn_in['Wk'], 'L0_xattn_Wv': _L0_xattn_in['Wv'], 'L0_xattn_bv': _L0_xattn_in['bv'], 'L0_xattn_Wq': _L0_xattn_in['Wq'], 'L0_xattn_bq': _L0_xattn_in['bq'], 'L0_xattn_Wo': _L0_xattn_in['Wo'], 'L0_xattn_bo': _L0_xattn_in['bo'], 'L0_ffn_router_w': _L0_ffn_in['router_w'], 'L0_ffn_expert_gate': _L0_ffn_in['expert_gate'], 'L0_ffn_expert_up': _L0_ffn_in['expert_up'], 'L0_ffn_expert_down': _L0_ffn_in['expert_down'], 'L0_ffn_shared_gate': _L0_ffn_in['shared_gate'], 'L0_ffn_shared_up': _L0_ffn_in['shared_up'], 'L0_ffn_shared_down': _L0_ffn_in['shared_down']}

def reference(x, ctx_1024, g_xattn, g_ffn, L0_xattn_Wk, L0_xattn_Wv, L0_xattn_bv, L0_xattn_Wq, L0_xattn_bq, L0_xattn_Wo, L0_xattn_bo, L0_ffn_router_w, L0_ffn_expert_gate, L0_ffn_expert_up, L0_ffn_expert_down, L0_ffn_shared_gate, L0_ffn_shared_up, L0_ffn_shared_down):
    import jax
    import jax.numpy as jnp

    def _L0_xattn_ref(k, v, q, Wk, Wv, bv, Wq, bq, Wo, bo):
        import jax, jax.numpy as jnp
        import numpy as np
        D_MODEL = 128
        B, S = (4, 256)
        kp = jnp.einsum('bsd,ed->bse', k, Wk)
        vp = jnp.einsum('bsd,ed->bse', v, Wv) + bv
        qp = jnp.einsum('bsd,ed->bse', q, Wq) + bq
        scale = 1.0 / jnp.sqrt(jnp.float32(kp.shape[-1]))
        scores = jnp.einsum('bqd,bkd->bqk', qp, kp) * scale
        probs = jax.nn.softmax(scores, axis=-1)
        ctx = jnp.einsum('bqk,bkd->bqd', probs, vp)
        return jnp.einsum('bqd,ed->bqe', ctx, Wo) + bo

    def _L0_ffn_ref(hidden_states, router_w, expert_gate, expert_up, expert_down, shared_gate, shared_up, shared_down):
        import jax, jax.numpy as jnp
        import numpy as np
        S, B, D, FF, E = (128, 2, 128, 256, 8)
        seq, bs, d = hidden_states.shape
        n_experts = expert_gate.shape[0]
        x = hidden_states.reshape(-1, d)
        logits = jnp.einsum('td,ed->te', x, router_w)
        top_logit = jnp.max(logits, axis=-1)
        top_idx = jnp.argmax(logits, axis=-1)
        score = jax.nn.sigmoid(top_logit)
        onehot = jax.nn.one_hot(top_idx, n_experts, dtype=x.dtype)
        xs = x * score[:, None]
        g = jnp.einsum('td,edf->etf', xs, expert_gate)
        u = jnp.einsum('td,edf->etf', xs, expert_up)
        h = jax.nn.silu(g) * u
        eo = jnp.einsum('etf,efd->etd', h, expert_down)
        moe_out = jnp.einsum('te,etd->td', onehot, eo)
        sh = jax.nn.silu(x @ shared_gate) * (x @ shared_up) @ shared_down
        return (moe_out + sh).reshape(seq, bs, d)
    x = x + jnp.tanh(g_xattn[0]) * _L0_xattn_ref(ctx_1024, ctx_1024, _layernorm(x, axis=-1), L0_xattn_Wk, L0_xattn_Wv, L0_xattn_bv, L0_xattn_Wq, L0_xattn_bq, L0_xattn_Wo, L0_xattn_bo)
    x = x + jnp.tanh(g_ffn[0]) * _L0_ffn_ref(_layernorm(x, axis=-1), L0_ffn_router_w, L0_ffn_expert_gate, L0_ffn_expert_up, L0_ffn_expert_down, L0_ffn_shared_gate, L0_ffn_shared_up, L0_ffn_shared_down)
    return x

_drawn_inputs = setup_inputs


def setup_inputs(seed=0):
    import zlib

    import numpy as np

    out = dict(_drawn_inputs(seed))
    spreads = {'L0_xattn_bv': (0.0, 0.1), 'L0_xattn_bq': (0.0, 0.431), 'L0_xattn_bo': (0.0, 0.1)}
    factors = {'L0_ffn_router_w': 8.0,
     'L0_ffn_expert_gate': 8.0,
     'L0_ffn_expert_up': 8.0,
     'L0_ffn_expert_down': 8.0,
     'L0_ffn_shared_gate': 8.0,
     'L0_ffn_shared_up': 7.941,
     'L0_ffn_shared_down': 7.992}
    for name, (base, spread) in spreads.items():
        noise = np.random.default_rng([zlib.crc32(name.encode()), seed]).standard_normal(out[name].shape)
        drawn = base * np.exp(spread * noise) if base else spread * noise
        out[name] = jnp.asarray(drawn.astype(out[name].dtype))
    for name, factor in factors.items():
        out[name] = (out[name] * factor).astype(out[name].dtype)
    return out
```

```python
import concourse.bass as bass
from concourse import mybir
from contextlib import ExitStack

F32 = mybir.dt.float32
F32R = mybir.dt.float32r
I32 = mybir.dt.int32
ALU = mybir.AluOpType
ACT = mybir.ActivationFunctionType
AX = mybir.AxisListType


def flamingo_layer(nc, x, ctx_t, ctx_n, ctx_tail, gates, wq, wk, wv, wo_t, bq, bv, bo,
                   router_t, expert_gu, expert_down, shared_gu, shared_down, out):
    B, D, NK = ctx_t.shape
    T = x.shape[1] // 128
    NT = B * T
    E = router_t.shape[1]
    FF = expert_down.shape[1]
    FC = FF // 128
    BANK = 512
    KC = -(-NK // 128)
    KF = NK // 128
    KR = NK - KF * 128
    SB = -(-NK // BANK)
    NKP = NK + NK % 2
    HALF = 2 * BANK
    SCALE = float(D) ** -0.5
    EPS = 1e-5
    ITEMS = 2 * (E + 1)
    assert D == 128 and T == 2 and SB == 4 and KC - KF == 1 and B % 2 == 0 and FC == 2

    ctx = ExitStack()
    with ctx:
        def sb(name, shape, dt=F32):
            return ctx.enter_context(nc.sbuf_tensor(name, shape, dt))

        def pb(name, shape, dt=F32):
            return ctx.enter_context(nc.psum_tensor(name, shape, dt))

        def sem(name):
            return ctx.enter_context(nc.semaphore(name))

        X = sb("X", [128, B, T, D])
        ctx_raw = [sb(f"ctx_raw{i}", [128, NKP]) for i in range(2)]
        ctx_hi = [sb(f"ctx_hi{i}", [128, NKP], F32R) for i in range(2)]
        ctx_lo = [sb(f"ctx_lo{i}", [128, NKP], F32R) for i in range(2)]
        ctx_rows = [sb(f"ctx_rows{i}", [128, KC, D]) for i in range(2)]
        probs = [sb(f"probs{i}", [128, NK]) for i in range(T)]
        probs_t = [sb(f"probs_t{i}", [128, KC, T, 128]) for i in range(2)]
        q_hi = [sb(f"q_hi{i}", [128, T * 128], F32R) for i in range(2)]
        q_lo = [sb(f"q_lo{i}", [128, T * 128], F32R) for i in range(2)]
        xn = sb("xn", [128, T, D])
        xn_t = sb("xn_t", [128, T * 128])
        o_t = sb("o_t", [128, T * 128])
        w_in = sb("w_in", [128, 4, D])
        m_qk = sb("m_qk", [128, D])
        c_qk = sb("c_qk", [128, 1])
        w_vo = sb("w_vo", [128, D])
        b_vo = sb("b_vo", [128, D])
        b_o = sb("b_o", [128, D])
        b_q = sb("b_q", [128, 1])
        b_v = sb("b_v", [128, 1])
        b_v_cols = sb("b_v_cols", [128, 128])
        g_raw = sb("g_raw", [128, 2])
        g_tanh = sb("g_tanh", [128, 2])
        ident = sb("ident", [128, 128])
        half_neg = sb("half_neg", [128, NT])
        stats = sb("stats", [128, T, 6])
        mv = sb("mv", [128, 2, T, 2])
        rstd = sb("rstd", [128, 2, T])
        stats2 = sb("stats2", [128, T, 6])
        mv2 = sb("mv2", [128, NT, 2])
        mv2_new = sb("mv2_new", [128, T, 2])
        rstd2 = sb("rstd2", [128, NT])
        mx = sb("mx", [128, 2, 2])
        neg_max = sb("neg_max", [128, 2])
        den = sb("den", [128, 2, T, 2])
        den_sum = sb("den_sum", [128, T])
        den_inv = sb("den_inv", [128, T])
        xn2 = sb("xn2", [128, 2, 4, D])
        xn2_t = sb("xn2_t", [128, NT, 128])
        w_gu = sb("w_gu", [128, 2 * FF * (E + 1)])
        w_down = sb("w_down", [128, (E + 1) * FC * D])
        w_router = sb("w_router", [128, E])
        rank_i = sb("rank_i", [128, NT, E], I32)
        rank_f = sb("rank_f", [128, NT, E])
        logits = sb("logits", [128, NT, E])
        tie = sb("tie", [128, NT, E])
        onehot = sb("onehot", [128, NT, E])
        top = sb("top", [128, NT])
        first = sb("first", [128, NT])
        score = sb("score", [128, NT + 1])
        weight = sb("weight", [128, NT, E])
        x_stage = [sb(f"x_stage{i}", [128, 128]) for i in range(2)]
        silu = [sb(f"silu{i}", [128, FF]) for i in range(2)]
        hid = [sb(f"hid{i}", [128, FF]) for i in range(2)]
        hid_t = [sb(f"hid_t{i}", [128, FC, 128]) for i in range(2)]
        res = [sb(f"res{i}", [128, D]) for i in range(2)]

        ps_s = pb("ps_s", [128, SB * BANK])
        ps_t = [pb(f"ps_t{i}", [128, BANK]) for i in range(2)]
        ps_o = pb("ps_o", [128, BANK])
        ps_q = pb("ps_q", [128, BANK])
        ps_gu = [ps_s[:, 0:BANK], ps_s[:, BANK:2 * BANK]]
        ps_ht = [ps_s[:, 2 * BANK:3 * BANK], ps_s[:, 3 * BANK:4 * BANK]]
        ps_y = ps_t

        names = ("ld_x ld_x_rest ld_w ld_ffn ctx_t_in0 ctx_t_in1 ctx_n_in0 ctx_n_in1 stored0 stored1 "
                 "settled const_ready pad_ready gates_ready bias_cols fold_done fold_ready "
                 "scores_done max_part neg_max_ready exp_done turned_done pt_act pt_dve "
                 "stats_part stats_ready veps_ready rstd_ready xn_ready xt_done xt_ready "
                 "query_done q_hi_ready q_lo_ready ctx_hi_ready ctx_lo_ready pv_done o_ready proj_done "
                 "den_part den_ready x_bias_ready x2_ready stats2_part mv2_part stats2_ready "
                 "veps2_ready rstd2_ready xn2_ready xn2_turned xn2_t_ready logits_done "
                 "logits_ready top_ready rank_ready x_staged route_step score_step weight_ready gu_done silu_ready hid_ready hid_turned hid_t_ready down_done res_ready").split()
        S = {n: sem(n) for n in names}

        block = ctx.enter_context(nc.Block())
        ctx_t_in = [S["ctx_t_in0"], S["ctx_t_in1"]]
        stored = [S["stored0"], S["stored1"]]
        ctx_n_in = [S["ctx_n_in0"], S["ctx_n_in1"]]

        def wait(eng, name, count):
            if type(count) is int and count <= 0:
                return
            eng.wait_ge(S[name] if type(name) is str else name, count)

        def settle(eng):
            eng.sem_inc(S["settled"], 1)

        def over_batches(eng, step):
            step(0, 0, 0, True, False)
            with eng.Fori(0, B // 2 - 1) as i:
                step(2 * i + 1, i, 1, False, False)
                step(2 * i + 2, i + 1, 0, False, False)
            step(B - 1, B // 2 - 1, 1, False, True)

        def repeat(eng, n, body):
            body(0)
            with eng.Fori(1, n) as i:
                body(i)

        @block.sync
        def _(sp):
            sp.dma_start(X[:, 0:2, :, :], x[0:2].rearrange("b (p t) d -> p b t d", t=T)).then_inc(S["ld_x"], 16)
            sp.dma_start(ctx_raw[0][:, 0:NK], ctx_t[0]).then_inc(ctx_t_in[0], 16)
            for n, w in enumerate((wq, wk, wv, wo_t)):
                sp.dma_start(w_in[:, n, :], w).then_inc(S["ld_w"], 16)
            sp.dma_start(b_q[:, :], bq.rearrange("(p o) -> p o", o=1)).then_inc(S["ld_w"], 16)
            sp.dma_start(b_v[:, :], bv.rearrange("(p o) -> p o", o=1)).then_inc(S["ld_w"], 16)
            sp.dma_start(b_o[:, :], bo.rearrange("(o d) -> o d", o=1).to_broadcast([128, D])).then_inc(S["ld_w"], 16)
            sp.dma_start(g_raw[:, :], gates.rearrange("(o d) -> o d", o=1).to_broadcast([128, 2])).then_inc(S["ld_w"], 16)
            sp.dma_start(X[:, 2:B, :, :], x[2:B].rearrange("b (p t) d -> p b t d", t=T)).then_inc(S["ld_x_rest"], 16)

            def load_rows(b, par):
                sp.dma_start(ctx_rows[par][:, 0:KF, :], ctx_n[b]).then_inc(ctx_n_in[par], 16)
                sp.dma_start(ctx_rows[par][0:KR, KF, :], ctx_tail[b]).then_inc(ctx_n_in[par], 16)

            load_rows(0, 0)
            sp.dma_start(ctx_raw[1][:, 0:NK], ctx_t[1]).then_inc(ctx_t_in[1], 16)
            load_rows(1, 1)
            sp.dma_start(w_router[:, :], router_t).then_inc(S["ld_ffn"], 16)
            sp.dma_start(w_gu[:, 0:2 * FF * E].rearrange("d (e f) -> d e f", e=E),
                         expert_gu).then_inc(S["ld_ffn"], 16)
            sp.dma_start(w_gu[:, 2 * FF * E:], shared_gu).then_inc(S["ld_ffn"], 16)
            for e in range(E):
                sp.dma_start(w_down[:, e * FC * D:(e + 1) * FC * D].rearrange("f (c d) -> f c d", c=FC),
                             expert_down[e].rearrange("(c f) d -> f c d", c=FC)).then_inc(S["ld_ffn"], 16)
            sp.dma_start(w_down[:, E * FC * D:].rearrange("f (c d) -> f c d", c=FC),
                         shared_down.rearrange("(c f) d -> f c d", c=FC)).then_inc(S["ld_ffn"], 16)
            with sp.Fori(1, B // 2) as i:
                for par in range(2):
                    b = 2 * i + par
                    wait(sp, "ctx_lo_ready", b - 1)
                    sp.dma_start(ctx_raw[par][:, 0:NK], ctx_t[b]).then_inc(ctx_t_in[par], 16)
                    wait(sp, "pv_done", b - 1)
                    sp.dma_start(ctx_rows[par][:, 0:KF, :], ctx_n[b]).then_inc(ctx_n_in[par], 16)
                    sp.dma_start(ctx_rows[par][0:KR, KF, :], ctx_tail[b]).then_inc(ctx_n_in[par], 16)
            out_v = out.rearrange("b (p t) d -> b t p d", t=T)

            def store(i):
                for t in range(T):
                    wait(sp, "res_ready", 2 * i + t + 1)
                    sp.dma_start(out_v[i, t], res[t][:, :]).then_inc(stored[t], 16)

            repeat(sp, B, store)
            for t in range(T):
                sp.wait_ge(stored[t], 16 * B)

        @block.gpsimd
        def _(pool):
            pool.memset(ident[:, :], 0.0).then_inc(S["const_ready"], 1)
            pool.memset(half_neg[:, :], -0.5).then_inc(S["const_ready"], 1)
            pool.memset(score[:, NT:NT + 1], 1.0).then_inc(S["const_ready"], 1)
            pool.iota(rank_i[:, :, :], pattern=[[0, NT], [-1, E]], base=E, channel_multiplier=0).then_inc(S["const_ready"], 1)
            pool.wait_ge(S["const_ready"], 4)
            pool.affine_select(out=ident[:, :], in_=ident[:, :], compare_op=ALU.not_equal, fill=1.0, base=0,
                               pattern=[[-1, 128]], channel_multiplier=1).then_inc(S["const_ready"], 1)

            def reciprocal_std(b, par):
                wait(pool, "stats_ready", b + 1)
                settle(pool)
                pool.tensor_scalar(mv[:, par, :, 1], mv[:, par, :, 1], EPS, None, ALU.add).then_inc(S["veps_ready"], 1)
                wait(pool, "veps_ready", b + 1)
                pool.tensor_tensor(rstd[:, par, :], mv[:, par, :, 1], half_neg[:, 0:T], ALU.pow).then_inc(S["rstd_ready"], 1)

            def low_part(b, par):
                wait(pool, "ctx_hi_ready", b + 1)
                pool.tensor_tensor(ctx_lo[par][:, 0:NK], ctx_raw[par][:, 0:NK], ctx_hi[par][:, 0:NK].bitcast(F32),
                                   ALU.subtract).then_inc(S["ctx_lo_ready"], 1)

            def add_bias(b):
                wait(pool, "xn_ready", b + 1)
                src = X[:, b, :, :]
                pool.tensor_tensor(src, src, b_vo[:, :].rearrange("p (o d) -> p o d", o=1).to_broadcast([128, T, D]),
                                   ALU.add).then_inc(S["x_bias_ready"], 1)

            def step(b, half, par, is_first, is_last):
                if is_last:
                    return
                reciprocal_std(b + 1, 1 - par)
                low_part(b + 1, 1 - par)
                add_bias(b + 1)

            reciprocal_std(0, 0)
            low_part(0, 0)
            pool.wait_ge(S["fold_ready"], 4)
            add_bias(0)
            over_batches(pool, step)

            pool.wait_ge(S["stats2_ready"], B)
            pool.tensor_scalar(mv2[:, :, 1], mv2[:, :, 1], EPS, None, ALU.add).then_inc(S["veps2_ready"], 1)
            pool.wait_ge(S["veps2_ready"], 1)
            pool.tensor_tensor(rstd2[:, :], mv2[:, :, 1], half_neg[:, :], ALU.pow).then_inc(S["rstd2_ready"], 1)

            pool.wait_ge(S["xn2_t_ready"], NT // 4)

            def stage(i):
                for t in range(2):
                    wait(pool, "gu_done", (E + 1) * (2 * i + t - 1))
                    pool.tensor_copy(x_stage[t][:, :], xn2_t[:, 2 * i + t, :]).then_inc(S["x_staged"], 1)

            repeat(pool, NT // 2, stage)

        @block.scalar
        def _(act):
            act.wait_ge(S["ld_w"], 16 * 8)
            act.activation(g_tanh[:, :], g_raw[:, :], ACT.Tanh).then_inc(S["gates_ready"], 1)

            def high_part(b, half, par):
                wait(act, ctx_t_in[par], 16 * half + 16)
                wait(act, "scores_done", 2 * SB * (b - 1))
                act.activation(ctx_hi[par][:, 0:NK], ctx_raw[par][:, 0:NK], ACT.Copy).then_inc(S["ctx_hi_ready"], 1)

            def keep_xn_t(b):
                wait(act, "xt_done", b + 1)
                wait(act, "query_done", b)
                act.activation(xn_t[:, :], ps_q[:, 0:T * 128], ACT.Copy).then_inc(S["xt_ready"], 1)

            def query_high(b, par):
                wait(act, "query_done", b + 1)
                wait(act, "scores_done", 2 * SB * (b - 1))
                act.activation(q_hi[par][:, :], ps_q[:, T * 128:], ACT.Identity, bias=c_qk[:, 0:1]).then_inc(S["q_hi_ready"], 1)

            def exponentials(b, par, t):
                tile = T * b + t
                wait(act, "neg_max_ready", tile + 1)
                wait(act, "turned_done", 4 * (tile - 1))
                for k, (lo, hi) in enumerate(((0, HALF), (HALF, NK))):
                    act.activation(probs[t][:, lo:hi], ps_s[:, lo:hi], ACT.Exp, bias=neg_max[:, t:t + 1],
                                   accum_out=den[:, par, t, k:k + 1]).then_inc(S["exp_done"], 1)

            def keep_turned(b, par, t):
                tile = T * b + t
                if t == 0:
                    wait(act, "pv_done", b - 1)
                for g in (0, 2):
                    wait(act, "turned_done", 4 * tile + g + 1)
                    act.activation(probs_t[par][:, 4 * g:4 * g + 4, t, :],
                                   ps_t[0][:, :].rearrange("p (c q) -> p c q", c=4), ACT.Copy).then_inc(S["pt_act"], 1)

            def keep_o(b):
                wait(act, "pv_done", b + 1)
                wait(act, "proj_done", b)
                act.activation(o_t[:, :], ps_o[:, 0:T * 128], ACT.Copy).then_inc(S["o_ready"], 1)

            def step(b, half, par, is_first, is_last):
                if not is_first:
                    keep_turned(b - 1, 1 - par, 1)
                exponentials(b, par, 0)
                if not is_last:
                    keep_xn_t(b + 1)
                    high_part(b + 1, half if par == 0 else half + 1, 1 - par)
                exponentials(b, par, 1)
                if not is_first:
                    keep_o(b - 1)
                if not is_last:
                    query_high(b + 1, 1 - par)
                keep_turned(b, par, 0)

            act.wait_ge(S["pad_ready"], 4)
            high_part(0, 0, 0)
            keep_xn_t(0)
            act.wait_ge(S["fold_ready"], 2)
            query_high(0, 0)
            over_batches(act, step)
            keep_turned(B - 1, 1, 1)
            keep_o(B - 1)

            def keep_xn2_t(i):
                for j in range(2):
                    n = 2 * i + j
                    wait(act, "xn2_turned", n + 1)
                    act.activation(xn2_t[:, bass.ds(4 * n, 4), :], ps_t[j][:, :].rearrange("p (c q) -> p c q", c=4),
                                   ACT.Copy).then_inc(S["xn2_t_ready"], 1)

            repeat(act, NT // 8, keep_xn2_t)
            act.wait_ge(S["top_ready"], 1)
            act.activation(score[:, 0:NT], top[:, :], ACT.Exp, scale=-1.0).then_inc(S["score_step"], 1)
            act.wait_ge(S["weight_ready"], 1)

            def experts(i):
                for m in range(ITEMS):
                    n, e, j, t = ITEMS * i + m, m % (E + 1), m % 2, m // (E + 1)
                    wait(act, "gu_done", n + 1)
                    settle(act)
                    sc = score[:, bass.ds(2 * i + t, 1)] if e < E else 1.0
                    act.activation(silu[j][:, :], ps_gu[j][:, 0:FF], ACT.Silu, scale=sc).then_inc(S["silu_ready"], 1)
                    wait(act, "hid_turned", n + 1)
                    act.activation(hid_t[j][:, :, :], ps_ht[j][:, 0:FF].rearrange("p (c q) -> p c q", c=FC),
                                   ACT.Copy).then_inc(S["hid_t_ready"], 1)

            repeat(act, NT // 2, experts)

        @block.vector
        def _(dve):
            for i in range(2):
                if NKP > NK:
                    dve.memset(ctx_hi[i][:, NK:NKP].bitcast(F32), 0.0).then_inc(S["pad_ready"], 1)
                    dve.memset(ctx_lo[i][:, NK:NKP].bitcast(F32), 0.0).then_inc(S["pad_ready"], 1)

            def statistics(b, par):
                xs = X[:, b, :, :]
                wait(dve, "stats_ready", b)
                settle(dve)
                for t in range(T):
                    dve.bn_stats(stats[:, t, :], xs[:, t, :]).then_inc(S["stats_part"], 1)
                wait(dve, "stats_part", T * b + T)
                wait(dve, "xn_ready", b - 1)
                settle(dve)
                for t in range(T):
                    last = dve.bn_aggr(mv[:, par, t, :], stats[:, t, :])
                last.then_inc(S["stats_ready"], 1)

            def normalize(b, par):
                xs = X[:, b, :, :]
                wait(dve, "rstd_ready", b + 1)
                wait(dve, "xt_done", b)
                for t in range(T):
                    last = dve.tensor_scalar(xn[:, t, :], xs[:, t, :], mv[:, par, t, 0:1], rstd[:, par, t:t + 1],
                                             ALU.subtract, ALU.mult)
                last.then_inc(S["xn_ready"], 1)

            def row_max(b, t):
                tile = T * b + t
                for k, (lo, hi) in enumerate(((0, HALF), (HALF, NK))):
                    wait(dve, "scores_done", SB * tile + 2 * k + 2)
                    dve.tensor_reduce(mx[:, t, k:k + 1], ps_s[:, lo:hi], AX.X, ALU.max, negate=True).then_inc(S["max_part"], 1)
                wait(dve, "max_part", 2 * tile + 2)
                dve.tensor_tensor(neg_max[:, t:t + 1], mx[:, t, 0:1], mx[:, t, 1:2], ALU.min).then_inc(S["neg_max_ready"], 1)

            def keep_turned(b, par, t):
                tile = T * b + t
                if t == 0:
                    wait(dve, "pv_done", b - 1)
                wait(dve, "turned_done", 4 * tile + 2)
                dve.tensor_copy(probs_t[par][:, 4:8, t, :], ps_t[1][:, :].rearrange("p (c q) -> p c q", c=4)).then_inc(S["pt_dve"], 1)
                wait(dve, "turned_done", 4 * tile + 4)
                dve.tensor_copy(probs_t[par][0:KR, KF, t, :], ps_t[1][0:KR, 0:128]).then_inc(S["pt_dve"], 1)

            def query_low(b, par):
                wait(dve, "q_hi_ready", b + 1)
                dve.scalar_tensor_tensor(out=q_lo[par][:, :], in0=ps_q[:, T * 128:], scalar=c_qk[:, 0:1],
                                         in1=q_hi[par][:, :].bitcast(F32), op0=ALU.add, op1=ALU.subtract).then_inc(S["q_lo_ready"], 1)

            def result(b, par):
                wait(dve, "exp_done", 2 * T * b + 2 * T)
                wait(dve, "x2_ready", b)
                dve.tensor_tensor(den_sum[:, :], den[:, par, :, 0], den[:, par, :, 1], ALU.add).then_inc(S["den_part"], 1)
                wait(dve, "den_part", b + 1)
                dve.reciprocal(den_inv[:, :], den_sum[:, :]).then_inc(S["den_ready"], 1)
                wait(dve, "den_ready", b + 1)
                wait(dve, "proj_done", b + 1)
                wait(dve, "x_bias_ready", b + 1)
                xs = X[:, b, :, :]
                for t in range(T):
                    last = dve.scalar_tensor_tensor(out=xs[:, t, :], in0=ps_o[:, (T + t) * 128:(T + t + 1) * 128],
                                                    scalar=den_inv[:, t:t + 1], in1=xs[:, t, :], op0=ALU.mult, op1=ALU.add)
                last.then_inc(S["x2_ready"], 1)
                wait(dve, "x2_ready", b + 1)
                wait(dve, "stats2_ready", b)
                settle(dve)
                for t in range(T):
                    last = dve.bn_stats(stats2[:, t, :], xs[:, t, :])
                last.then_inc(S["stats2_part"], 1)
                wait(dve, "stats2_part", b + 1)
                settle(dve)
                for t in range(T):
                    last = dve.bn_aggr(mv2_new[:, t, :], stats2[:, t, :])
                last.then_inc(S["mv2_part"], 1)
                wait(dve, "mv2_part", b + 1)
                settle(dve)
                dve.tensor_copy(mv2[:, bass.ds(T * b, T), :], mv2_new[:, :, :]).then_inc(S["stats2_ready"], 1)

            def step(b, half, par, is_first, is_last):
                row_max(b, 0)
                if not is_last:
                    statistics(b + 1, 1 - par)
                if not is_first:
                    keep_turned(b - 1, 1 - par, 1)
                if not is_last:
                    normalize(b + 1, 1 - par)
                row_max(b, 1)
                if not is_last:
                    query_low(b + 1, 1 - par)
                keep_turned(b, par, 0)
                if not is_first:
                    result(b - 1, 1 - par)

            dve.wait_ge(S["ld_x"], 16)
            statistics(0, 0)
            normalize(0, 0)
            dve.wait_ge(S["ld_w"], 16 * 8)
            dve.tensor_copy(b_v_cols[:, :], b_v[:, 0:1].to_broadcast([128, 128])).then_inc(S["bias_cols"], 1)
            dve.wait_ge(S["fold_done"], 1)
            dve.tensor_scalar(m_qk[:, :], ps_o[:, 0:128], SCALE, None, ALU.mult).then_inc(S["fold_ready"], 1)
            dve.tensor_scalar(c_qk[:, :], ps_o[:, 384:385], SCALE, None, ALU.mult).then_inc(S["fold_ready"], 1)
            dve.wait_ge(S["gates_ready"], 1)
            dve.tensor_scalar(w_vo[:, :], ps_o[:, 128:256], g_tanh[:, 0:1], None, ALU.mult).then_inc(S["fold_ready"], 1)
            dve.tensor_tensor(b_vo[:, :], ps_o[:, 256:384], b_o[:, :], ALU.add).then_inc(S["bias_cols"], 1)
            dve.wait_ge(S["bias_cols"], 2)
            dve.tensor_scalar(b_vo[:, :], b_vo[:, :], g_tanh[:, 0:1], None, ALU.mult).then_inc(S["fold_ready"], 1)
            query_low(0, 0)
            dve.wait_ge(S["ld_x_rest"], 16)
            over_batches(dve, step)
            keep_turned(B - 1, 1, 1)
            result(B - 1, 1)

            dve.wait_ge(S["const_ready"], 5)
            dve.tensor_copy(rank_f[:, :, :], rank_i[:, :, :]).then_inc(S["rank_ready"], 1)
            dve.wait_ge(S["rstd2_ready"], 1)

            def normalize2(i):
                for j in range(2):
                    n = 2 * i + j
                    wait(dve, "xn2_turned", n - 1)
                    for t in range(4):
                        tile = 4 * n + t
                        last = dve.tensor_scalar(xn2[:, j, t, :], X[:, 2 * n + t // 2, t % 2, :],
                                                 mv2[:, tile, 0:1], rstd2[:, bass.ds(tile, 1)],
                                                 ALU.subtract, ALU.mult)
                    last.then_inc(S["xn2_ready"], 1)

            repeat(dve, NT // 8, normalize2)

            def bcast(v):
                return v.rearrange("p (n o) -> p n o", o=1).to_broadcast([128, NT, E])

            dve.wait_ge(S["logits_done"], 1)
            dve.tensor_copy(logits[:, :, :], ps_q[:, 0:NT * E].rearrange("p (n e) -> p n e", e=E)).then_inc(S["logits_ready"], 1)
            dve.wait_ge(S["logits_ready"], 1)
            dve.tensor_reduce(top[:, :], logits[:, :, :], AX.X, ALU.max).then_inc(S["top_ready"], 1)
            dve.wait_ge(S["top_ready"], 1)
            dve.tensor_tensor(tie[:, :, :], logits[:, :, :], bcast(top[:, :]), ALU.is_equal).then_inc(S["route_step"], 1)
            dve.wait_ge(S["route_step"], 1)
            dve.wait_ge(S["rank_ready"], 1)
            dve.tensor_tensor(tie[:, :, :], tie[:, :, :], rank_f[:, :, :], ALU.mult).then_inc(S["route_step"], 1)
            dve.wait_ge(S["route_step"], 2)
            dve.tensor_reduce(first[:, :], tie[:, :, :], AX.X, ALU.max).then_inc(S["route_step"], 1)
            dve.wait_ge(S["route_step"], 3)
            dve.tensor_tensor(onehot[:, :, :], tie[:, :, :], bcast(first[:, :]), ALU.is_equal).then_inc(S["route_step"], 1)
            dve.wait_ge(S["score_step"], 1)
            dve.tensor_scalar(score[:, 0:NT], score[:, 0:NT], 1.0, None, ALU.add).then_inc(S["score_step"], 1)
            dve.wait_ge(S["score_step"], 2)
            dve.reciprocal(score[:, 0:NT], score[:, 0:NT]).then_inc(S["score_step"], 1)
            dve.wait_ge(S["score_step"], 3)
            dve.wait_ge(S["route_step"], 4)
            dve.tensor_tensor(weight[:, :, :], onehot[:, :, :], bcast(score[:, 0:NT]), ALU.mult).then_inc(S["weight_ready"], 1)
            dve.wait_ge(S["weight_ready"], 1)

            def experts(i):
                for m in range(ITEMS):
                    n, e, j, t = ITEMS * i + m, m % (E + 1), m % 2, m // (E + 1)
                    tile = 2 * i + t
                    wait(dve, "silu_ready", n + 1)
                    w = weight[:, tile, e:e + 1] if e < E else score[:, NT:NT + 1]
                    dve.scalar_tensor_tensor(out=hid[j][:, :], in0=ps_gu[j][:, FF:2 * FF], scalar=w, in1=silu[j][:, :],
                                             op0=ALU.mult, op1=ALU.mult).then_inc(S["hid_ready"], 1)
                    if e == E:
                        wait(dve, "down_done", tile + 1)
                        wait(dve, stored[t], 16 * i)
                        dve.scalar_tensor_tensor(out=res[t][:, :], in0=ps_y[t][:, 0:D], scalar=g_tanh[:, 1:2],
                                                 in1=X[:, i, t, :], op0=ALU.mult, op1=ALU.add).then_inc(S["res_ready"], 1)

            repeat(dve, NT // 2, experts)

        @block.tensor
        def _(pe):
            pe.wait_ge(S["ld_w"], 16 * 8)
            pe.wait_ge(S["bias_cols"], 1)
            pe.matmul(ps_o[:, 0:128], w_in[:, 0, :], w_in[:, 1, :], start=True, stop=True)
            pe.matmul(ps_o[:, 128:256], w_in[:, 2, :], w_in[:, 3, :], start=True, stop=True)
            pe.matmul(ps_o[:, 256:384], b_v_cols[:, :], w_in[:, 3, :], start=True, stop=True)
            pe.matmul(ps_o[:, 384:385], w_in[:, 1, :], b_q[:, :], start=True, stop=True).then_inc(S["fold_done"], 1)

            def turn_x(b):
                wait(pe, "xn_ready", b + 1)
                wait(pe, "q_lo_ready", b)
                for t in range(T):
                    last = pe.transpose(ps_q[:, t * 128:(t + 1) * 128], xn[:, t, :], ident[:, :])
                last.then_inc(S["xt_done"], 1)

            def query(b):
                wait(pe, "xt_ready", b + 1)
                pe.matmul(ps_q[:, T * 128:], m_qk[:, :], xn_t[:, :], start=True, stop=True).then_inc(S["query_done"], 1)

            def scores(b, par, t):
                tile = T * b + t
                wait(pe, "ctx_lo_ready", b + 1)
                wait(pe, "q_lo_ready", b + 1)
                qs = slice(t * 128, (t + 1) * 128)
                for k in range(SB):
                    cols = slice(k * BANK, min((k + 1) * BANK, NKP))
                    if k % 2 == 0:
                        wait(pe, "exp_done", 2 * (tile - 1) + k // 2 + 1)
                    o = ps_s[:, cols]
                    pe.matmul(o, q_hi[par][:, qs], ctx_hi[par][:, cols], start=True, stop=False)
                    pe.matmul(o, q_hi[par][:, qs], ctx_lo[par][:, cols], start=False, stop=False)
                    pe.matmul(o, q_lo[par][:, qs], ctx_hi[par][:, cols], start=False, stop=True).then_inc(S["scores_done"], 1)

            def turn_probs(b, t):
                tile = T * b + t
                for g in range(4):
                    if g % 2 == 0:
                        wait(pe, "exp_done", 2 * tile + g // 2 + 1)
                    wait(pe, "pt_act" if g % 2 == 0 else "pt_dve", 2 * tile + g // 2)
                    for c in range(4 * g, min(4 * g + 4, KC)):
                        n = min(128, NK - c * 128)
                        last = pe.transpose(ps_t[g % 2][0:n, (c % 4) * 128:(c % 4 + 1) * 128],
                                            probs[t][:, c * 128:c * 128 + n], ident[:, :])
                    last.then_inc(S["turned_done"], 1)

            def weigh(b, half, par, chunks):
                tile = T * b + 1
                for c in chunks:
                    if c == 0:
                        wait(pe, ctx_n_in[par], 32 * half + 32)
                        wait(pe, "x2_ready", b)
                    if c % 4 == 0:
                        wait(pe, "pt_act" if c % 8 == 0 else "pt_dve", 2 * tile + c // 8 + 1)
                    n = min(128, NK - c * 128)
                    last = pe.matmul(ps_o[:, 0:T * 128], ctx_rows[par][0:n, c, :],
                                     probs_t[par][0:n, c, :, :].rearrange("p t q -> p (t q)"), start=(c == 0), stop=(c == KC - 1))
                if chunks[-1] == KC - 1:
                    last.then_inc(S["pv_done"], 1)

            def project(b):
                wait(pe, "o_ready", b + 1)
                for t in range(T):
                    last = pe.matmul(ps_o[:, (T + t) * 128:(T + t + 1) * 128], o_t[:, t * 128:(t + 1) * 128], w_vo[:, :],
                                     start=True, stop=True)
                last.then_inc(S["proj_done"], 1)

            def step(b, half, par, is_first, is_last):
                before = half if par == 1 else half - 1
                scores(b, par, 0)
                if not is_first:
                    turn_probs(b - 1, 1)
                    weigh(b - 1, before, 1 - par, range(0, 7))
                if not is_last:
                    turn_x(b + 1)
                scores(b, par, 1)
                if not is_first:
                    weigh(b - 1, before, 1 - par, range(7, KC))
                if not is_last:
                    query(b + 1)
                turn_probs(b, 0)
                if not is_first:
                    project(b - 1)

            pe.wait_ge(S["const_ready"], 5)
            turn_x(0)
            pe.wait_ge(S["fold_ready"], 4)
            query(0)
            over_batches(pe, step)
            turn_probs(B - 1, 1)
            weigh(B - 1, B // 2 - 1, 1, range(0, KC))
            project(B - 1)

            def turn_xn2(i):
                for j in range(2):
                    n = 2 * i + j
                    wait(pe, "xn2_ready", n + 1)
                    wait(pe, "xn2_t_ready", n - 1)
                    for t in range(4):
                        last = pe.transpose(ps_t[j][:, t * 128:(t + 1) * 128], xn2[:, j, t, :], ident[:, :])
                    last.then_inc(S["xn2_turned"], 1)

            repeat(pe, NT // 8, turn_xn2)
            pe.wait_ge(S["xn2_t_ready"], NT // 4)
            pe.wait_ge(S["ld_ffn"], 16 * (4 + E))
            for tile in range(NT):
                last = pe.matmul(ps_q[:, tile * E:(tile + 1) * E], xn2_t[:, tile, :], w_router[:, :], start=True, stop=True)
            last.then_inc(S["logits_done"], 1)

            def gate_up(i, m):
                e, j, t = m % (E + 1), m % 2, m // (E + 1)
                if e == 0:
                    wait(pe, "x_staged", 2 * i + t + 1)
                pe.matmul(ps_gu[j], x_stage[t][:, :], w_gu[:, e * 2 * FF:(e + 1) * 2 * FF],
                          start=True, stop=True).then_inc(S["gu_done"], 1)

            def experts(i):
                gate_up(i, 0)
                for m in range(ITEMS):
                    n, e, j, t = ITEMS * i + m, m % (E + 1), m % 2, m // (E + 1)
                    if m + 1 < ITEMS:
                        gate_up(i, m + 1)
                    wait(pe, "hid_ready", n + 1)
                    for c in range(FC):
                        last = pe.transpose(ps_ht[j][:, c * 128:(c + 1) * 128], hid[j][:, c * 128:(c + 1) * 128], ident[:, :])
                    last.then_inc(S["hid_turned"], 1)
                    wait(pe, "hid_t_ready", n + 1)
                    if e == 0:
                        wait(pe, "res_ready", 2 * i + t - 1)
                    for c in range(FC):
                        w = (e * FC + c) * D
                        last = pe.matmul(ps_y[t][:, 0:D], hid_t[j][:, c, :], w_down[:, w:w + D],
                                         start=(e == 0 and c == 0), stop=(e == E and c == FC - 1))
                    if e == E:
                        last.then_inc(S["down_done"], 1)

            repeat(pe, NT // 2, experts)


def kernel(**inputs):
    import numpy as np
    import concourse.bacc as bacc
    from concourse.bass_utils import run_bass_kernel_spmd as run

    g = {k: np.asarray(v) for k, v in inputs.items()}
    ctx = g["ctx_1024"]
    B, NK, D = ctx.shape
    full = NK // 128 * 128
    arrays = {
        "x": g["x"],
        "ctx_t": ctx.transpose(0, 2, 1),
        "ctx_n": ctx[:, :full].reshape(B, full // 128, 128, D).transpose(0, 2, 1, 3),
        "ctx_tail": ctx[:, full:],
        "gates": np.concatenate([g["g_xattn"], g["g_ffn"]]),
        "wq": g["L0_xattn_Wq"], "wk": g["L0_xattn_Wk"], "wv": g["L0_xattn_Wv"], "wo_t": g["L0_xattn_Wo"].T,
        "bq": g["L0_xattn_bq"], "bv": g["L0_xattn_bv"], "bo": g["L0_xattn_bo"],
        "router_t": g["L0_ffn_router_w"].T,
        "expert_gu": np.concatenate([g["L0_ffn_expert_gate"], g["L0_ffn_expert_up"]], axis=2).transpose(1, 0, 2),
        "expert_down": g["L0_ffn_expert_down"],
        "shared_gu": np.concatenate([g["L0_ffn_shared_gate"], g["L0_ffn_shared_up"]], axis=1),
        "shared_down": g["L0_ffn_shared_down"],
    }
    arrays = {k: np.ascontiguousarray(v) for k, v in arrays.items()}
    nc = bacc.Bacc("TRN2", target_bir_lowering=False, num_devices=1)
    args = [nc.dram_tensor(k, v.shape, mybir.dt.from_np(v.dtype), kind="ExternalInput").ap() for k, v in arrays.items()]
    out = nc.dram_tensor("out", g["x"].shape, F32, kind="ExternalOutput").ap()
    flamingo_layer(nc, *args, out)
    return run(nc, [arrays], core_ids=[0]).results[0]["out"]
```

```python
import concourse.bass as bass
from concourse import mybir
from contextlib import ExitStack

F32 = mybir.dt.float32
F32R = mybir.dt.float32r
I32 = mybir.dt.int32
U32 = mybir.dt.uint32
ALU = mybir.AluOpType
ACT = mybir.ActivationFunctionType
AX = mybir.AxisListType


def flamingo_layer(nc, x, ctx_t, ctx_n, ctx_tail, gates, wq, wk, wv, wo_t, bq, bv, bo,
                   router_t, expert_gu, expert_down, shared_gu, shared_down, out):
    B, D, NK = ctx_t.shape
    T = x.shape[1] // 128
    NT = B * T
    E = router_t.shape[1]
    FF = expert_down.shape[1]
    FC = FF // 128
    BANK = 512
    KC = -(-NK // 128)
    KF = NK // 128
    KR = NK - KF * 128
    SB = -(-NK // BANK)
    NKP = NK + NK % 2
    HALF = 2 * BANK
    SCALE = float(D) ** -0.5
    EPS = 1e-5
    REGION = NT + 1
    NJ = NT + E - 1
    SPARE = NJ - NT
    ROWS = (E * REGION + SPARE) * 128
    EARLY = 8
    DEPTH = 4
    assert D == 128 and T == 2 and SB == 4 and KC - KF == 1 and B % 2 == 0 and FC == 2 and EARLY % 2 == 0

    sorted_x = nc.dram_tensor("sorted_x", (ROWS, D), F32).ap()
    sorted_y = nc.dram_tensor("sorted_y", (NJ * 128, D), F32).ap()

    ctx = ExitStack()
    with ctx:
        def sb(name, shape, dt=F32):
            return ctx.enter_context(nc.sbuf_tensor(name, shape, dt))

        def pb(name, shape, dt=F32):
            return ctx.enter_context(nc.psum_tensor(name, shape, dt))

        X = sb("X", [128, B, T, D])
        ctx_raw = [sb(f"ctx_raw{i}", [128, NKP]) for i in range(2)]
        ctx_hi = [sb(f"ctx_hi{i}", [128, NKP], F32R) for i in range(2)]
        ctx_lo = [sb(f"ctx_lo{i}", [128, NKP], F32R) for i in range(2)]
        ctx_rows = [sb(f"ctx_rows{i}", [128, KC, D]) for i in range(2)]
        probs = [sb(f"probs{i}", [128, NK]) for i in range(T)]
        probs_t = [sb(f"probs_t{i}", [128, KC, T, 128]) for i in range(2)]
        q_hi = [sb(f"q_hi{i}", [128, T * 128], F32R) for i in range(2)]
        q_lo = [sb(f"q_lo{i}", [128, T * 128], F32R) for i in range(2)]
        xn = sb("xn", [128, T, D])
        xn_t = sb("xn_t", [128, T * 128])
        o_t = sb("o_t", [128, T * 128])
        w_in = sb("w_in", [128, 4, D])
        m_qk = sb("m_qk", [128, D])
        c_qk = sb("c_qk", [128, 1])
        w_vo = sb("w_vo", [128, D])
        b_vo = sb("b_vo", [128, D])
        b_o = sb("b_o", [128, D])
        b_q = sb("b_q", [128, 1])
        b_v = sb("b_v", [128, 1])
        b_v_cols = sb("b_v_cols", [128, 128])
        g_raw = sb("g_raw", [128, 2])
        g_tanh = sb("g_tanh", [128, 2])
        ident = sb("ident", [128, 128])
        ones = sb("ones", [128, 128])
        zeros = sb("zeros", [128, 128])
        before = sb("before", [128, 128])
        powers = sb("powers", [128, 2, T])
        stats = sb("stats", [128, T, 6])
        mv = sb("mv", [128, 2, T, 2])
        rstd = sb("rstd", [128, 2, T])
        stats2 = sb("stats2", [128, T, 6])
        mv2 = sb("mv2", [128, 2, T, 2])
        rstd2 = sb("rstd2", [128, 2, T])
        mx = sb("mx", [128, 2, 2])
        neg_max = sb("neg_max", [128, 2])
        den = sb("den", [128, 2, T, 2])
        den_sum = sb("den_sum", [128, T])
        den_inv = sb("den_inv", [128, T])
        xn2 = [sb(f"xn2_{i}", [128, T, D]) for i in range(2)]
        xn2_new = sb("xn2_new", [128, T * 128])
        xn2_t = sb("xn2_t", [128, NT, 128])
        rank_i = sb("rank_i", [128, T, E], I32)
        rank_f = sb("rank_f", [128, T, E])
        region_i = sb("region_i", [128, T, E], I32)
        region_f = sb("region_f", [128, T, E])
        top = sb("top", [128, 2, T])
        tie = sb("tie", [128, T, E])
        first = sb("first", [128, T])
        onehot = sb("onehot", [128, 2, T, E])
        seen = sb("seen", [128, T, E])
        place = sb("place", [128, T, E])
        row_f = sb("row_f", [128, T])
        row_new = [sb(f"row_new{i}", [128, T], U32) for i in range(2)]
        onehots = sb("onehots", [128, NT, E])
        rows = sb("rows", [128, NT])
        shift = sb("shift", [128, E])
        row_shift = sb("row_shift", [128, NT])
        row_of = sb("row_of", [128, NT], U32)
        e_top = sb("e_top", [128, T])
        score = sb("score", [128, T])
        xs = [sb(f"xs{i}", [128, T, D]) for i in range(2)]
        count_f = sb("count_f", [128, E])
        count_i = sb("count_i", [128, E], I32)
        tiles = sb("tiles", [128, E])
        tiles_end = sb("tiles_end", [128, E])
        slot_i = sb("slot_i", [128, NJ, 1], I32)
        slot_f = sb("slot_f", [128, NJ, 1])
        past = sb("past", [128, NJ, E])
        past_tiles = sb("past_tiles", [128, NJ, E])
        slot_expert = sb("slot_expert", [128, NJ])
        slot_base = sb("slot_base", [128, NJ])
        slot_tile = sb("slot_tile", [128, NJ])
        slot_tile_i = sb("slot_tile_i", [128, NJ], I32)
        slot_weight_i = sb("slot_weight_i", [128, NJ], I32)
        w_gu = sb("w_gu", [128, 2 * FF * (E + 1)])
        w_down = sb("w_down", [128, (E + 1) * FC * D])
        w_router = sb("w_router", [128, E])
        x_sorted = [sb(f"x_sorted{i}", [128, D]) for i in range(DEPTH)]
        y_sorted = [sb(f"y_sorted{i}", [128, D]) for i in range(DEPTH)]
        x_stage = [sb(f"x_stage{i}", [128, 128]) for i in range(2)]
        silu = [sb(f"silu{i}", [128, FF]) for i in range(2)]
        hid = [sb(f"hid{i}", [128, FF]) for i in range(2)]
        hid_t = [sb(f"hid_t{i}", [128, FC, 128]) for i in range(2)]
        y_token = sb("y_token", [128, NT, D])

        ps_s = pb("ps_s", [128, SB * BANK])
        ps_t = [pb(f"ps_t{i}", [128, BANK]) for i in range(2)]
        ps_o = pb("ps_o", [128, BANK])
        ps_q = pb("ps_q", [128, BANK])
        ps_place = ps_q[:, 256:256 + T * E].rearrange("p (t e) -> p t e", e=E)
        ps_logit = ps_q[:, 256 + T * E:256 + 2 * T * E].rearrange("p (t e) -> p t e", e=E)
        ps_count = ps_q[:, 256 + 2 * T * E:256 + 2 * T * E + E]
        ps_gu = [ps_s[:, 0:BANK], ps_s[:, BANK:2 * BANK]]
        ps_ht = [ps_s[:, 2 * BANK:3 * BANK], ps_s[:, 3 * BANK:4 * BANK]]
        ps_y = ps_t
        ps_x = [ps_q, ps_o]

        names = ("ld_x ld_x_rest ld_w ld_ffn pads_stored zeros_stored "
                 "settled const_ready matrix_ready pad_ready gates_ready bias_cols fold_done fold_ready "
                 "scores_done max_part neg_max_ready exp_done turned_done pt_act pt_dve "
                 "stats_part stats_ready veps_ready rstd_ready xn_ready xt_done xt_ready "
                 "query_done q_hi_ready q_lo_ready ctx_hi_ready ctx_lo_ready pv_done o_ready proj_done "
                 "den_part den_ready x_bias_ready x2_ready stats2_part stats2_ready "
                 "veps2_ready rstd2_ready xn2_ready xn2_turned xn2_new_ready xn2_t_ready logits_done "
                 "rank_ready top_ready route_step onehot_ready seen_step seen_ready places_done place_step row_ready kept_rows rows_final "
                 "e_top_ready score_part score_ready xs_ready counted table_step table_ready "
                 "x_staged xs_turned gu_done silu_ready hid_ready hid_turned hid_t_ready down_done y_kept out_ready stored").split()
        S = {n: ctx.enter_context(nc.semaphore(n)) for n in names}

        def ring(name, n):
            return [ctx.enter_context(nc.semaphore(f"{name}{i}")) for i in range(n)]

        ctx_t_in = ring("ctx_t_in", 2)
        ctx_n_in = ring("ctx_n_in", 2)
        scattered = ring("scattered", 2)
        x_sorted_in = ring("x_sorted_in", DEPTH)
        y_sorted_out = ring("y_sorted_out", DEPTH)
        gathered = ring("gathered", 2)

        block = ctx.enter_context(nc.Block())

        def wait(eng, name, count):
            if type(count) is int and count <= 0:
                return
            eng.wait_ge(S[name] if type(name) is str else name, count)

        def settle(eng):
            eng.sem_inc(S["settled"], 1)

        def over_batches(eng, step):
            def alone(b):
                step(b, b // 2, b % 2, lambda k: 0 <= b + k < B)

            for b in range(3):
                alone(b)
            with eng.Fori(0, B // 2 - 2) as i:
                step(2 * i + 3, i + 1, 1, lambda k: True)
                step(2 * i + 4, i + 2, 0, lambda k: True)
            for b in range(B - 1, B + 3):
                alone(b)

        SEGMENTS = [(0, EARLY, 0, False), (EARLY, NJ, 0, True), (EARLY + NJ, NT - EARLY, EARLY, False)]

        def over_items(eng, count, step):
            def alone(m):
                step(m, m // DEPTH, m % DEPTH, lambda k: 0 <= m + k < count)

            looped = max(0, (count - 1) // DEPTH - 2)
            for m in range(2 * DEPTH):
                alone(m)
            if looped:
                with eng.Fori(2, 2 + looped) as i:
                    for k in range(DEPTH):
                        step(DEPTH * i + k, i, k, lambda n: True)
            for m in range(DEPTH * (2 + looped), count + 2):
                alone(m)

        @block.sync
        def _(sp):
            sp.dma_start(X[:, 0:2, :, :], x[0:2].rearrange("b (p t) d -> p b t d", t=T)).then_inc(S["ld_x"], 16)
            sp.dma_start(ctx_raw[0][:, 0:NK], ctx_t[0]).then_inc(ctx_t_in[0], 16)
            for n, w in enumerate((wq, wk, wv, wo_t)):
                sp.dma_start(w_in[:, n, :], w).then_inc(S["ld_w"], 16)
            sp.dma_start(b_q[:, :], bq.rearrange("(p o) -> p o", o=1)).then_inc(S["ld_w"], 16)
            sp.dma_start(b_v[:, :], bv.rearrange("(p o) -> p o", o=1)).then_inc(S["ld_w"], 16)
            sp.dma_start(b_o[:, :], bo.rearrange("(o d) -> o d", o=1).to_broadcast([128, D])).then_inc(S["ld_w"], 16)
            sp.dma_start(g_raw[:, :], gates.rearrange("(o d) -> o d", o=1).to_broadcast([128, 2])).then_inc(S["ld_w"], 16)
            sp.dma_start(w_router[:, :], router_t).then_inc(S["ld_w"], 16)

            def load_rows(b, par):
                sp.dma_start(ctx_rows[par][:, 0:KF, :], ctx_n[b]).then_inc(ctx_n_in[par], 16)
                sp.dma_start(ctx_rows[par][0:KR, KF, :], ctx_tail[b]).then_inc(ctx_n_in[par], 16)

            sp.dma_start(ctx_raw[1][:, 0:NK], ctx_t[1]).then_inc(ctx_t_in[1], 16)
            load_rows(0, 0)
            sp.dma_start(X[:, 2:B, :, :], x[2:B].rearrange("b (p t) d -> p b t d", t=T)).then_inc(S["ld_x_rest"], 16)
            load_rows(1, 1)
            sp.wait_ge(S["const_ready"], 8)
            for n in range(SPARE):
                at = (E * REGION + n) * 128
                sp.dma_start(sorted_x[at:at + 128, :], zeros[:, :]).then_inc(S["zeros_stored"], 16)

            def load_context(b, par):
                wait(sp, "ctx_lo_ready", b - 1)
                sp.dma_start(ctx_raw[par][:, 0:NK], ctx_t[b]).then_inc(ctx_t_in[par], 16)
                wait(sp, "pv_done", b - 1)
                load_rows(b, par)

            for b in range(2, 4):
                load_context(b, b % 2)
            sp.dma_start(w_gu[:, 0:2 * FF * E].rearrange("d (e f) -> d e f", e=E), expert_gu).then_inc(S["ld_ffn"], 16)
            sp.dma_start(w_gu[:, 2 * FF * E:], shared_gu).then_inc(S["ld_ffn"], 16)
            for e in range(E):
                sp.dma_start(w_down[:, e * FC * D:(e + 1) * FC * D].rearrange("f (c d) -> f c d", c=FC),
                             expert_down[e].rearrange("(c f) d -> f c d", c=FC)).then_inc(S["ld_ffn"], 16)
            sp.dma_start(w_down[:, E * FC * D:].rearrange("f (c d) -> f c d", c=FC),
                         shared_down.rearrange("(c f) d -> f c d", c=FC)).then_inc(S["ld_ffn"], 16)
            with sp.Fori(2, B // 2) as i:
                for par in range(2):
                    load_context(2 * i + par, par)

            sp.wait_ge(S["table_ready"], 1)
            for e in range(E):
                n = sp.value_load(count_i[0:1, e:e + 1], min_val=0, max_val=NT * 128)
                sp.dma_start(sorted_x[bass.ds(n + e * REGION * 128, 128), :], zeros[:, :]).then_inc(S["pads_stored"], 16)
            sp.wait_ge(S["table_ready"], 3)
            for par in range(2):
                sp.wait_ge(scattered[par], 16 * NT // 2)
            sp.wait_ge(S["zeros_stored"], 16 * SPARE)
            sp.wait_ge(S["pads_stored"], 16 * E)

            def load_sorted(j, k):
                row = sp.value_load(slot_tile_i[0:1, bass.ds(j, 1)], min_val=0, max_val=ROWS // 128 - 1)
                sp.dma_start(x_sorted[k][:, :], sorted_x[bass.ds(row * 128, 128), :]).then_inc(x_sorted_in[k], 16)

            def store_sorted(j, k):
                wait(sp, "y_kept", EARLY + j + 1)
                settle(sp)
                sp.dma_start(sorted_y[bass.ds(j * 128, 128), :], y_sorted[k][:, :]).then_inc(y_sorted_out[k], 16)

            for j in range(DEPTH):
                load_sorted(j, j)

            def turn_around(j, k):
                if type(j) is not int or j + DEPTH < NJ:
                    wait(sp, "xs_turned", j + 1)
                    settle(sp)
                    load_sorted(j + DEPTH, k)
                if type(j) is not int or j >= 2:
                    store_sorted(j - 2, (k - 2) % DEPTH)

            for j in range(DEPTH):
                turn_around(j, j)
            looped = (NJ - DEPTH) // DEPTH - 1
            with sp.Fori(1, 1 + looped) as i:
                for k in range(DEPTH):
                    turn_around(DEPTH * i + k, k)
            for j in range(DEPTH * (1 + looped), NJ + 2):
                turn_around(j, j % DEPTH)

            out_v = out.rearrange("b (p t) d -> b p t d", t=T)
            with sp.Fori(0, B) as b:
                wait(sp, "out_ready", T * b + T)
                sp.dma_start(out_v[b], X[:, b, :, :]).then_inc(S["stored"], 16)
            sp.wait_ge(S["stored"], 16 * B)

        @block.gpsimd
        def _(pool):
            pool.memset(ident[:, :], 0.0).then_inc(S["const_ready"], 1)
            pool.memset(ones[:, :], 1.0).then_inc(S["const_ready"], 1)
            pool.memset(zeros[:, :], 0.0).then_inc(S["const_ready"], 1)
            pool.memset(before[:, :], 1.0).then_inc(S["const_ready"], 1)
            pool.memset(powers[:, 0, :], -0.5).then_inc(S["const_ready"], 1)
            pool.memset(powers[:, 1, :], -1.0).then_inc(S["const_ready"], 1)
            pool.iota(rank_i[:, :, :], pattern=[[0, T], [-1, E]], base=E, channel_multiplier=0).then_inc(S["const_ready"], 1)
            pool.iota(slot_i[:, :, :], pattern=[[1, NJ], [0, 1]], base=0, channel_multiplier=0).then_inc(S["const_ready"], 1)
            pool.iota(region_i[:, :, :], pattern=[[0, T], [REGION * 128, E]], base=0, channel_multiplier=0).then_inc(S["matrix_ready"], 1)
            pool.wait_ge(S["const_ready"], 8)
            pool.affine_select(out=ident[:, :], in_=ident[:, :], compare_op=ALU.not_equal, fill=1.0, base=0,
                               pattern=[[-1, 128]], channel_multiplier=1).then_inc(S["matrix_ready"], 1)
            pool.affine_select(out=before[:, :], in_=before[:, :], compare_op=ALU.is_gt, fill=0.0, base=0,
                               pattern=[[1, 128]], channel_multiplier=-1).then_inc(S["matrix_ready"], 1)

            def reciprocal_std(b, par):
                wait(pool, "stats_ready", b + 1)
                settle(pool)
                pool.tensor_scalar(mv[:, par, :, 1], mv[:, par, :, 1], EPS, None, ALU.add).then_inc(S["veps_ready"], 1)
                wait(pool, "veps_ready", b + 1)
                pool.tensor_tensor(rstd[:, par, :], mv[:, par, :, 1], powers[:, 0, :], ALU.pow).then_inc(S["rstd_ready"], 1)

            def reciprocal_std2(b, par):
                wait(pool, "stats2_ready", b + 1)
                settle(pool)
                pool.tensor_scalar(mv2[:, par, :, 1], mv2[:, par, :, 1], EPS, None, ALU.add).then_inc(S["veps2_ready"], 1)
                wait(pool, "veps2_ready", b + 1)
                pool.tensor_tensor(rstd2[:, par, :], mv2[:, par, :, 1], powers[:, 0, :], ALU.pow).then_inc(S["rstd2_ready"], 1)

            def low_part(b, par):
                wait(pool, "ctx_hi_ready", b + 1)
                pool.tensor_tensor(ctx_lo[par][:, 0:NK], ctx_raw[par][:, 0:NK], ctx_hi[par][:, 0:NK].bitcast(F32),
                                   ALU.subtract).then_inc(S["ctx_lo_ready"], 1)

            def add_bias(b):
                wait(pool, "xn_ready", b + 1)
                settle(pool)
                pool.tensor_tensor(X[:, b, :, :], X[:, b, :, :],
                                   b_vo[:, :].rearrange("p (o d) -> p o d", o=1).to_broadcast([128, T, D]),
                                   ALU.add).then_inc(S["x_bias_ready"], 1)

            def scatter(b, half, par):
                wait(pool, "e_top_ready", b + 1)
                settle(pool)
                pool.tensor_scalar(e_top[:, :], e_top[:, :], 1.0, None, ALU.add).then_inc(S["score_part"], 1)
                wait(pool, "score_part", b + 1)
                pool.tensor_tensor(score[:, :], e_top[:, :], powers[:, 1, :], ALU.pow).then_inc(S["score_ready"], 1)
                wait(pool, "score_ready", b + 1)
                wait(pool, scattered[par], 16 * T * half)
                pool.tensor_tensor(xs[par][:, :, :], xn2[par][:, :, :],
                                   score[:, :].rearrange("p (t o) -> p t o", o=1).to_broadcast([128, T, D]),
                                   ALU.mult).then_inc(S["xs_ready"], 1)
                wait(pool, "row_ready", b + 1)
                wait(pool, "xs_ready", b + 1)
                settle(pool)
                for t in range(T):
                    pool.indirect_dma_start(sorted_x[:, :], bass.IndirectOffsetOnAxis(row_new[par][:, t:t + 1], 0),
                                            xs[par][:, t, :], None).then_inc(scattered[par], 16)

            def step(b, half, par, has):
                if has(-2):
                    reciprocal_std2(b - 2, par)
                if has(1):
                    reciprocal_std(b + 1, 1 - par)
                    low_part(b + 1, 1 - par)
                    add_bias(b + 1)
                if has(-3):
                    scatter(b - 3, half + (par - 3) // 2, 1 - par)

            reciprocal_std(0, 0)
            low_part(0, 0)
            pool.wait_ge(S["fold_ready"], 4)
            add_bias(0)
            over_batches(pool, step)

            pool.wait_ge(S["rows_final"], 1)
            for k in range(DEPTH):
                pool.wait_ge(y_sorted_out[k], 16 * len(range(k, NJ, DEPTH)))
            for n in range(NT):
                wait(pool, gathered[n % 2], 16 * (n // 2))
                pool.indirect_dma_start(y_token[:, n, :], None, sorted_y[:, :],
                                        bass.IndirectOffsetOnAxis(row_of[:, n:n + 1], 0)).then_inc(gathered[n % 2], 16)

        @block.scalar
        def _(act):
            act.wait_ge(S["ld_w"], 16 * 9)
            act.activation(g_tanh[:, :], g_raw[:, :], ACT.Tanh).then_inc(S["gates_ready"], 1)

            def high_part(b, half, par):
                wait(act, ctx_t_in[par], 16 * half + 16)
                wait(act, "scores_done", 2 * SB * (b - 1))
                act.activation(ctx_hi[par][:, 0:NK], ctx_raw[par][:, 0:NK], ACT.Copy).then_inc(S["ctx_hi_ready"], 1)

            def keep_xn_t(b):
                wait(act, "xt_done", b + 1)
                wait(act, "query_done", b)
                act.activation(xn_t[:, :], ps_q[:, 0:T * 128], ACT.Copy).then_inc(S["xt_ready"], 1)

            def query_high(b, par):
                wait(act, "query_done", b + 1)
                wait(act, "scores_done", 2 * SB * (b - 1))
                act.activation(q_hi[par][:, :], ps_q[:, T * 128:], ACT.Identity, bias=c_qk[:, 0:1]).then_inc(S["q_hi_ready"], 1)

            def exponentials(b, par, t):
                tile = T * b + t
                wait(act, "neg_max_ready", tile + 1)
                wait(act, "turned_done", 4 * (tile - 1))
                for k, (lo, hi) in enumerate(((0, HALF), (HALF, NK))):
                    act.activation(probs[t][:, lo:hi], ps_s[:, lo:hi], ACT.Exp, bias=neg_max[:, t:t + 1],
                                   accum_out=den[:, par, t, k:k + 1]).then_inc(S["exp_done"], 1)

            def keep_turned(b, par, t, g):
                if t == 0:
                    wait(act, "pv_done", b - 1)
                wait(act, "turned_done", 4 * (T * b + t) + g + 1)
                act.activation(probs_t[par][:, 4 * g:4 * g + 4, t, :],
                               ps_t[0][:, :].rearrange("p (c q) -> p c q", c=4), ACT.Copy).then_inc(S["pt_act"], 1)

            def keep_o(b):
                wait(act, "pv_done", b + 1)
                wait(act, "proj_done", b)
                act.activation(o_t[:, :], ps_o[:, 0:T * 128], ACT.Copy).then_inc(S["o_ready"], 1)

            def keep_xn2_t(b):
                wait(act, "xn2_turned", b + 1)
                wait(act, "logits_done", b)
                act.activation(xn2_new[:, :], ps_q[:, 0:T * 128], ACT.Copy).then_inc(S["xn2_new_ready"], 1)
                act.activation(xn2_t[:, bass.ds(T * b, T), :], ps_q[:, 0:T * 128].rearrange("p (t q) -> p t q", t=T),
                               ACT.Copy).then_inc(S["xn2_t_ready"], 1)

            def exp_top(b, par):
                wait(act, "top_ready", b + 1)
                wait(act, "score_ready", b)
                act.activation(e_top[:, :], top[:, par, :], ACT.Exp, scale=-1.0).then_inc(S["e_top_ready"], 1)

            def step(b, half, par, has):
                if has(-1):
                    keep_turned(b - 1, 1 - par, 1, 0)
                    keep_turned(b - 1, 1 - par, 1, 2)
                if has(0):
                    exponentials(b, par, 0)
                if has(-3):
                    exp_top(b - 3, 1 - par)
                if has(1):
                    high_part(b + 1, half + (par + 1) // 2, 1 - par)
                if has(-2):
                    keep_xn2_t(b - 2)
                if has(0):
                    keep_turned(b, par, 0, 0)
                    keep_turned(b, par, 0, 2)
                if has(1):
                    keep_xn_t(b + 1)
                if has(0):
                    exponentials(b, par, 1)
                if has(1):
                    query_high(b + 1, 1 - par)
                if has(-1):
                    keep_o(b - 1)

            act.wait_ge(S["pad_ready"], 5)
            high_part(0, 0, 0)
            keep_xn_t(0)
            act.wait_ge(S["fold_ready"], 2)
            query_high(0, 0)
            over_batches(act, step)

            for base, count, _, _ in SEGMENTS:
                def item(m, group, k, has):
                    j = k % 2
                    if has(0):
                        wait(act, "gu_done", base + m + 1)
                        act.activation(silu[j][:, :], ps_gu[j][:, 0:FF], ACT.Silu).then_inc(S["silu_ready"], 1)
                    if has(-1):
                        wait(act, "hid_turned", base + m)
                        act.activation(hid_t[1 - j][:, :, :], ps_ht[1 - j][:, 0:FF].rearrange("p (c q) -> p c q", c=FC),
                                       ACT.Copy).then_inc(S["hid_t_ready"], 1)

                over_items(act, count, item)

        @block.vector
        def _(dve):
            for i in range(2):
                dve.memset(ctx_hi[i][:, NK:NKP].bitcast(F32), 0.0).then_inc(S["pad_ready"], 1)
                dve.memset(ctx_lo[i][:, NK:NKP].bitcast(F32), 0.0).then_inc(S["pad_ready"], 1)
            dve.memset(seen[:, :, :], 0.0).then_inc(S["pad_ready"], 1)

            def statistics(b, par):
                wait(dve, "stats_ready", b)
                settle(dve)
                for t in range(T):
                    last = dve.bn_stats(stats[:, t, :], X[:, b, t, :])
                last.then_inc(S["stats_part"], 1)
                wait(dve, "stats_part", b + 1)
                wait(dve, "xn_ready", b - 1)
                settle(dve)
                for t in range(T):
                    last = dve.bn_aggr(mv[:, par, t, :], stats[:, t, :])
                last.then_inc(S["stats_ready"], 1)

            def normalize(b, par):
                wait(dve, "rstd_ready", b + 1)
                wait(dve, "xt_done", b)
                for t in range(T):
                    last = dve.tensor_scalar(xn[:, t, :], X[:, b, t, :], mv[:, par, t, 0:1], rstd[:, par, t:t + 1],
                                             ALU.subtract, ALU.mult)
                last.then_inc(S["xn_ready"], 1)

            def part_max(b, t, k):
                tile = T * b + t
                lo, hi = ((0, HALF), (HALF, NK))[k]
                wait(dve, "scores_done", SB * tile + 2 * k + 2)
                dve.tensor_reduce(mx[:, t, k:k + 1], ps_s[:, lo:hi], AX.X, ALU.max, negate=True).then_inc(S["max_part"], 1)
                if k == 1:
                    wait(dve, "max_part", 2 * tile + 2)
                    dve.tensor_tensor(neg_max[:, t:t + 1], mx[:, t, 0:1], mx[:, t, 1:2], ALU.min).then_inc(S["neg_max_ready"], 1)

            def keep_turned(b, par, t, g):
                if t == 0:
                    wait(dve, "pv_done", b - 1)
                wait(dve, "turned_done", 4 * (T * b + t) + g + 1)
                if g == 1:
                    dve.tensor_copy(probs_t[par][:, 4:8, t, :], ps_t[1][:, :].rearrange("p (c q) -> p c q", c=4)).then_inc(S["pt_dve"], 1)
                else:
                    dve.tensor_copy(probs_t[par][0:KR, KF, t, :], ps_t[1][0:KR, 0:128]).then_inc(S["pt_dve"], 1)

            def query_low(b, par):
                wait(dve, "q_hi_ready", b + 1)
                dve.scalar_tensor_tensor(out=q_lo[par][:, :], in0=ps_q[:, T * 128:], scalar=c_qk[:, 0:1],
                                         in1=q_hi[par][:, :].bitcast(F32), op0=ALU.add, op1=ALU.subtract).then_inc(S["q_lo_ready"], 1)

            def result(b, par):
                wait(dve, "exp_done", 2 * T * b + 2 * T)
                wait(dve, "x2_ready", b)
                dve.tensor_tensor(den_sum[:, :], den[:, par, :, 0], den[:, par, :, 1], ALU.add).then_inc(S["den_part"], 1)
                wait(dve, "den_part", b + 1)
                dve.reciprocal(den_inv[:, :], den_sum[:, :]).then_inc(S["den_ready"], 1)
                wait(dve, "den_ready", b + 1)
                wait(dve, "proj_done", b + 1)
                wait(dve, "x_bias_ready", b + 1)
                for t in range(T):
                    last = dve.scalar_tensor_tensor(out=X[:, b, t, :], in0=ps_o[:, (T + t) * 128:(T + t + 1) * 128],
                                                    scalar=den_inv[:, t:t + 1], in1=X[:, b, t, :], op0=ALU.mult, op1=ALU.add)
                last.then_inc(S["x2_ready"], 1)

            def statistics2(b, par):
                wait(dve, "x2_ready", b + 1)
                wait(dve, "stats2_ready", b)
                settle(dve)
                for t in range(T):
                    last = dve.bn_stats(stats2[:, t, :], X[:, b, t, :])
                last.then_inc(S["stats2_part"], 1)
                wait(dve, "stats2_part", b + 1)
                wait(dve, "xn2_ready", b - 1)
                settle(dve)
                for t in range(T):
                    last = dve.bn_aggr(mv2[:, par, t, :], stats2[:, t, :])
                last.then_inc(S["stats2_ready"], 1)

            def normalize2(b, par):
                wait(dve, "rstd2_ready", b + 1)
                wait(dve, "xn2_turned", b - 1)
                wait(dve, "xs_ready", b - 1)
                for t in range(T):
                    last = dve.tensor_scalar(xn2[par][:, t, :], X[:, b, t, :], mv2[:, par, t, 0:1], rstd2[:, par, t:t + 1],
                                             ALU.subtract, ALU.mult)
                last.then_inc(S["xn2_ready"], 1)

            def bcast(v):
                return v.rearrange("p (t o) -> p t o", o=1).to_broadcast([128, T, E])

            def find_top(b, par):
                wait(dve, "logits_done", b + 1)
                wait(dve, "e_top_ready", b - 1)
                dve.tensor_reduce(top[:, par, :], ps_logit, AX.X, ALU.max).then_inc(S["top_ready"], 1)
                wait(dve, "top_ready", b + 1)
                wait(dve, "route_step", 3 * b)
                dve.tensor_tensor(tie[:, :, :], ps_logit, bcast(top[:, par, :]), ALU.is_equal).then_inc(S["route_step"], 1)

            def choose(b, par):
                wait(dve, "route_step", 3 * b + 1)
                dve.tensor_tensor(tie[:, :, :], tie[:, :, :], rank_f[:, :, :], ALU.mult).then_inc(S["route_step"], 1)
                wait(dve, "route_step", 3 * b + 2)
                dve.tensor_reduce(first[:, :], tie[:, :, :], AX.X, ALU.max).then_inc(S["route_step"], 1)
                wait(dve, "route_step", 3 * b + 3)
                dve.tensor_tensor(onehot[:, par, :, :], tie[:, :, :], bcast(first[:, :]), ALU.is_equal).then_inc(S["onehot_ready"], 1)
                wait(dve, "onehot_ready", b + 1)
                wait(dve, "seen_step", b)
                dve.tensor_tensor(seen[:, 1, :], seen[:, 0, :], onehot[:, par, 0, :], ALU.add).then_inc(S["seen_ready"], 1)

            def find_place(b, par):
                wait(dve, "places_done", b + 1)
                wait(dve, "xn2_t_ready", b + 2 if type(b) is not int else min(b + 2, B))
                dve.tensor_tensor(place[:, :, :], ps_place, region_f[:, :, :], ALU.add).then_inc(S["place_step"], 1)
                wait(dve, "place_step", 3 * b + 1)
                dve.tensor_tensor(place[:, :, :], place[:, :, :], onehot[:, par, :, :], ALU.mult).then_inc(S["place_step"], 1)
                wait(dve, "place_step", 3 * b + 2)
                dve.tensor_reduce(row_f[:, :], place[:, :, :], AX.X, ALU.add).then_inc(S["place_step"], 1)
                wait(dve, "place_step", 3 * b + 3)
                wait(dve, scattered[par], 16 * T * b_half(b))
                dve.tensor_copy(row_new[par][:, :], row_f[:, :]).then_inc(S["row_ready"], 1)
                dve.tensor_tensor(seen[:, 0, :], seen[:, 1, :], onehot[:, par, 1, :], ALU.add).then_inc(S["seen_step"], 1)
                wait(dve, "row_ready", b + 1)
                settle(dve)
                dve.tensor_copy(onehots[:, bass.ds(T * b, T), :], onehot[:, par, :, :]).then_inc(S["kept_rows"], 1)
                dve.tensor_copy(rows[:, bass.ds(T * b, T)], row_f[:, :]).then_inc(S["kept_rows"], 1)

            halves = {}

            def b_half(b):
                return halves["place"]

            def step(b, half, par, has):
                halves["place"] = half + (par - 3) // 2
                if has(0):
                    part_max(b, 0, 0)
                if has(-1):
                    keep_turned(b - 1, 1 - par, 1, 1)
                if has(0):
                    part_max(b, 0, 1)
                if has(-1):
                    keep_turned(b - 1, 1 - par, 1, 3)
                if has(-2):
                    normalize2(b - 2, par)
                if has(1):
                    statistics(b + 1, 1 - par)
                    normalize(b + 1, 1 - par)
                if has(0):
                    part_max(b, 1, 0)
                    keep_turned(b, par, 0, 1)
                if has(-3):
                    find_place(b - 3, 1 - par)
                if has(-2):
                    find_top(b - 2, par)
                if has(0):
                    part_max(b, 1, 1)
                    keep_turned(b, par, 0, 3)
                if has(-2):
                    choose(b - 2, par)
                if has(1):
                    query_low(b + 1, 1 - par)
                if has(-1):
                    result(b - 1, 1 - par)
                    statistics2(b - 1, 1 - par)

            dve.wait_ge(S["ld_x"], 16)
            statistics(0, 0)
            normalize(0, 0)
            dve.wait_ge(S["ld_w"], 16 * 9)
            dve.tensor_copy(b_v_cols[:, :], b_v[:, 0:1].to_broadcast([128, 128])).then_inc(S["bias_cols"], 1)
            dve.wait_ge(S["fold_done"], 1)
            dve.tensor_scalar(m_qk[:, :], ps_o[:, 0:128], SCALE, None, ALU.mult).then_inc(S["fold_ready"], 1)
            dve.tensor_scalar(c_qk[:, :], ps_o[:, 384:385], SCALE, None, ALU.mult).then_inc(S["fold_ready"], 1)
            dve.wait_ge(S["gates_ready"], 1)
            dve.tensor_scalar(w_vo[:, :], ps_o[:, 128:256], g_tanh[:, 0:1], None, ALU.mult).then_inc(S["fold_ready"], 1)
            dve.tensor_tensor(b_vo[:, :], ps_o[:, 256:384], b_o[:, :], ALU.add).then_inc(S["bias_cols"], 1)
            dve.wait_ge(S["bias_cols"], 2)
            dve.tensor_scalar(b_vo[:, :], b_vo[:, :], g_tanh[:, 0:1], None, ALU.mult).then_inc(S["fold_ready"], 1)
            query_low(0, 0)
            dve.wait_ge(S["matrix_ready"], 3)
            dve.tensor_copy(rank_f[:, :, :], rank_i[:, :, :]).then_inc(S["rank_ready"], 1)
            dve.tensor_copy(region_f[:, :, :], region_i[:, :, :]).then_inc(S["rank_ready"], 1)
            dve.tensor_copy(slot_f[:, :, :], slot_i[:, :, :]).then_inc(S["rank_ready"], 1)
            dve.wait_ge(S["rank_ready"], 3)
            dve.wait_ge(S["ld_x_rest"], 16)
            over_batches(dve, step)

            steps = [0]

            def table(op):
                wait(dve, "table_step", steps[0])
                op().then_inc(S["table_step"], 1)
                steps[0] += 1

            def by_slot(v):
                return v.to_broadcast([128, NJ, E])

            def by_expert(v):
                return v.rearrange("p (o e) -> p o e", o=1).to_broadcast([128, NJ, E])

            def slots(v):
                return v.rearrange("p (j o) -> p j o", o=1)

            def tables():
                dve.wait_ge(S["counted"], 1)
                dve.tensor_copy(count_i[:, :], ps_count).then_inc(S["table_ready"], 1)
                table(lambda: dve.tensor_copy(count_f[:, :], ps_count))
                table(lambda: dve.scalar_tensor_tensor(out=past[:, :, :], in0=by_slot(slot_f[:, :, :]), scalar=128.0,
                                                       in1=by_expert(count_f[:, :]), op0=ALU.mult, op1=ALU.is_lt))
                table(lambda: dve.tensor_reduce(tiles[:, :], past[:, :, :].rearrange("p j e -> p e j"), AX.X, ALU.add))
                table(lambda: dve.tensor_copy(tiles_end[:, 0:1], tiles[:, 0:1]))
                for e in range(1, E):
                    table(lambda: dve.tensor_tensor(tiles_end[:, e:e + 1], tiles_end[:, e - 1:e], tiles[:, e:e + 1], ALU.add))
                table(lambda: dve.tensor_tensor(past[:, :, :], by_slot(slot_f[:, :, :]), by_expert(tiles_end[:, :]), ALU.is_ge))
                table(lambda: dve.tensor_reduce(slot_expert[:, :], past[:, :, :], AX.X, ALU.add))
                table(lambda: dve.tensor_tensor(past[:, :, :], past[:, :, :], by_expert(tiles[:, :]), ALU.mult))
                table(lambda: dve.tensor_reduce(slot_base[:, :], past[:, :, :], AX.X, ALU.add))
                table(lambda: dve.scalar_tensor_tensor(out=slot_tile[:, :], in0=slot_expert[:, :], scalar=float(REGION),
                                                       in1=slot_base[:, :], op0=ALU.mult, op1=ALU.subtract))
                table(lambda: dve.tensor_tensor(slot_tile[:, :], slot_tile[:, :], slot_f[:, :, :].rearrange("p j o -> p (j o)"), ALU.add))
                table(lambda: dve.tensor_scalar(slot_expert[:, :], slot_expert[:, :], float(E - 1), None, ALU.min))
                dve.wait_ge(S["table_step"], steps[0])
                dve.tensor_copy(slot_tile_i[:, :], slot_tile[:, :]).then_inc(S["table_ready"], 1)
                dve.tensor_copy(slot_weight_i[:, :], slot_expert[:, :]).then_inc(S["table_ready"], 1)

            def result_rows():
                dve.wait_ge(S["kept_rows"], 2 * B)
                table(lambda: dve.tensor_tensor(shift[:, :], tiles_end[:, :], tiles[:, :], ALU.subtract))
                table(lambda: dve.scalar_tensor_tensor(out=shift[:, :], in0=shift[:, :], scalar=128.0, in1=region_f[:, 0, :],
                                                       op0=ALU.mult, op1=ALU.subtract))
                table(lambda: dve.tensor_tensor(onehots[:, :, :], onehots[:, :, :],
                                                shift[:, :].rearrange("p (o e) -> p o e", o=1).to_broadcast([128, NT, E]), ALU.mult))
                table(lambda: dve.tensor_reduce(row_shift[:, :], onehots[:, :, :], AX.X, ALU.add))
                table(lambda: dve.tensor_tensor(rows[:, :], rows[:, :], row_shift[:, :], ALU.add))
                dve.wait_ge(S["table_step"], steps[0])
                dve.tensor_copy(row_of[:, :], rows[:, :]).then_inc(S["rows_final"], 1)

            x_tiles = X[:, :, :, :].rearrange("p b t d -> p (b t) d")

            def stage_shared(n, tile, j, used):
                wait(dve, "gu_done", used)
                settle(dve)
                dve.tensor_copy(x_stage[j][:, :], xn2_t[:, tile, :]).then_inc(S["x_staged"], 1)

            def stage_sorted(m, j, used):
                wait(dve, "gu_done", used)
                wait(dve, "xs_turned", m + 1)
                dve.tensor_copy(x_stage[j][:, :], ps_x[j][:, 0:128]).then_inc(S["x_staged"], 1)

            def add_experts(n, par, pair):
                wait(dve, gathered[par], 16 * (pair + 1))
                wait(dve, "y_kept", NJ + n + 1)
                settle(dve)
                dve.scalar_tensor_tensor(out=x_tiles[:, n, :], in0=y_token[:, n, :], scalar=g_tanh[:, 1:2],
                                         in1=x_tiles[:, n, :], op0=ALU.mult, op1=ALU.add).then_inc(S["out_ready"], 1)

            def feed_forward(base, count, tile0, experts, finish):
                def item(m, group, k, has):
                    j = k % 2
                    if has(1):
                        if experts:
                            stage_sorted(m + 1, 1 - j, base + m)
                        else:
                            stage_shared(base + m + 1, tile0 + m + 1, 1 - j, base + m)
                    if has(0):
                        wait(dve, "silu_ready", base + m + 1)
                        dve.tensor_tensor(hid[j][:, :], ps_gu[j][:, FF:2 * FF], silu[j][:, :], ALU.mult).then_inc(S["hid_ready"], 1)
                    if has(-2):
                        wait(dve, "down_done", base + m - 1)
                        if experts:
                            wait(dve, y_sorted_out[(k - 2) % DEPTH], 16 * (group + (k - 2) // DEPTH))
                            dve.tensor_copy(y_sorted[(k - 2) % DEPTH][:, :], ps_y[j][:, 0:D]).then_inc(S["y_kept"], 1)
                        else:
                            settle(dve)
                            dve.scalar_tensor_tensor(out=x_tiles[:, tile0 + m - 2, :], in0=ps_y[j][:, 0:D], scalar=g_tanh[:, 1:2],
                                                     in1=x_tiles[:, tile0 + m - 2, :], op0=ALU.mult,
                                                     op1=ALU.add).then_inc(S["y_kept"], 1)
                    if finish and has(-2 * DEPTH):
                        add_experts(m - 2 * DEPTH, j, 2 * group - DEPTH + k // 2)

                if experts:
                    stage_sorted(0, 0, base)
                else:
                    stage_shared(base, tile0, 0, base)
                over_items(dve, count, item)

            feed_forward(*SEGMENTS[0], False)
            tables()
            feed_forward(*SEGMENTS[1], False)
            result_rows()
            feed_forward(*SEGMENTS[2], True)
            for n in range(NT - EARLY - 2 * DEPTH + 2, NT):
                add_experts(n, n % 2, n // 2)

        @block.tensor
        def _(pe):
            pe.wait_ge(S["ld_w"], 16 * 9)
            pe.wait_ge(S["bias_cols"], 1)
            pe.matmul(ps_o[:, 0:128], w_in[:, 0, :], w_in[:, 1, :], start=True, stop=True)
            pe.matmul(ps_o[:, 128:256], w_in[:, 2, :], w_in[:, 3, :], start=True, stop=True)
            pe.matmul(ps_o[:, 256:384], b_v_cols[:, :], w_in[:, 3, :], start=True, stop=True)
            pe.matmul(ps_o[:, 384:385], w_in[:, 1, :], b_q[:, :], start=True, stop=True).then_inc(S["fold_done"], 1)

            def turn_x(b):
                wait(pe, "xn_ready", b + 1)
                wait(pe, "q_lo_ready", b)
                wait(pe, "route_step", 3 * (b - 3) + 1)
                for t in range(T):
                    last = pe.transpose(ps_q[:, t * 128:(t + 1) * 128], xn[:, t, :], ident[:, :])
                last.then_inc(S["xt_done"], 1)

            def query(b):
                wait(pe, "xt_ready", b + 1)
                pe.matmul(ps_q[:, T * 128:], m_qk[:, :], xn_t[:, :], start=True, stop=True).then_inc(S["query_done"], 1)

            def scores(b, par, t, k):
                tile = T * b + t
                if t == 0 and k == 0:
                    wait(pe, "ctx_lo_ready", b + 1)
                    wait(pe, "q_lo_ready", b + 1)
                if k % 2 == 0:
                    wait(pe, "exp_done", 2 * (tile - 1) + k // 2 + 1)
                cols = slice(k * BANK, min((k + 1) * BANK, NKP))
                qs = slice(t * 128, (t + 1) * 128)
                o = ps_s[:, cols]
                pe.matmul(o, q_hi[par][:, qs], ctx_hi[par][:, cols], start=True, stop=False)
                pe.matmul(o, q_hi[par][:, qs], ctx_lo[par][:, cols], start=False, stop=False)
                pe.matmul(o, q_lo[par][:, qs], ctx_hi[par][:, cols], start=False, stop=True).then_inc(S["scores_done"], 1)

            def turn_probs(b, t, g):
                tile = T * b + t
                if g % 2 == 0:
                    wait(pe, "exp_done", 2 * tile + g // 2 + 1)
                wait(pe, "pt_act" if g % 2 == 0 else "pt_dve", 2 * tile + g // 2)
                for c in range(4 * g, min(4 * g + 4, KC)):
                    n = min(128, NK - c * 128)
                    last = pe.transpose(ps_t[g % 2][0:n, (c % 4) * 128:(c % 4 + 1) * 128],
                                        probs[t][:, c * 128:c * 128 + n], ident[:, :])
                last.then_inc(S["turned_done"], 1)

            def weigh(b, half, par, chunks):
                tile = T * b + 1
                for c in chunks:
                    if c == 0:
                        wait(pe, ctx_n_in[par], 32 * half + 32)
                        wait(pe, "x2_ready", b)
                    if c % 4 == 0:
                        wait(pe, "pt_act" if c % 8 == 0 else "pt_dve", 2 * tile + c // 8 + 1)
                    n = min(128, NK - c * 128)
                    last = pe.matmul(ps_o[:, 0:T * 128], ctx_rows[par][0:n, c, :],
                                     probs_t[par][0:n, c, :, :].rearrange("p t q -> p (t q)"), start=(c == 0), stop=(c == KC - 1))
                if chunks[-1] == KC - 1:
                    last.then_inc(S["pv_done"], 1)

            def project(b):
                wait(pe, "o_ready", b + 1)
                for t in range(T):
                    last = pe.matmul(ps_o[:, (T + t) * 128:(T + t + 1) * 128], o_t[:, t * 128:(t + 1) * 128], w_vo[:, :],
                                     start=True, stop=True)
                last.then_inc(S["proj_done"], 1)

            def flat(v):
                return v.rearrange("p t e -> p (t e)")

            def places(b, par):
                wait(pe, "seen_ready", b + 1)
                pe.matmul(flat(ps_place), ones[:, :], flat(seen[:, :, :]), start=True, stop=False)
                pe.matmul(flat(ps_place), before[:, :], flat(onehot[:, par, :, :]), start=False, stop=True).then_inc(S["places_done"], 1)

            def turn_xn2(b, par):
                wait(pe, "xn2_ready", b + 1)
                for t in range(T):
                    last = pe.transpose(ps_q[:, t * 128:(t + 1) * 128], xn2[par][:, t, :], ident[:, :])
                last.then_inc(S["xn2_turned"], 1)

            def logits(b):
                wait(pe, "xn2_new_ready", b + 1)
                wait(pe, "xn2_t_ready", b + 1)
                wait(pe, "place_step", 3 * (b - 1) + 1)
                for t in range(T):
                    last = pe.matmul(ps_logit[:, t, :], xn2_new[:, t * 128:(t + 1) * 128], w_router[:, :], start=True, stop=True)
                last.then_inc(S["logits_done"], 1)

            def step(b, half, par, has):
                earlier = half + (par - 1) // 2
                for k in range(SB):
                    if has(0):
                        scores(b, par, 0, k)
                    if has(-1):
                        turn_probs(b - 1, 1, k)
                if has(-1):
                    weigh(b - 1, earlier, 1 - par, range(0, 7))
                if has(-3):
                    places(b - 3, 1 - par)
                if has(-2):
                    turn_xn2(b - 2, par)
                for k in range(SB):
                    if has(0):
                        scores(b, par, 1, k)
                        turn_probs(b, 0, k)
                    if k == 1 and has(-2):
                        logits(b - 2)
                if has(1):
                    turn_x(b + 1)
                if has(-1):
                    weigh(b - 1, earlier, 1 - par, range(7, 10))
                if has(1):
                    query(b + 1)
                if has(-1):
                    weigh(b - 1, earlier, 1 - par, range(10, KC))
                    project(b - 1)

            pe.wait_ge(S["matrix_ready"], 3)
            turn_x(0)
            pe.wait_ge(S["fold_ready"], 4)
            query(0)
            over_batches(pe, step)
            pe.wait_ge(S["seen_step"], B)
            pe.matmul(ps_count, ones[:, :], seen[:, 0, :], start=True, stop=True).then_inc(S["counted"], 1)

            pe.wait_ge(S["ld_ffn"], 16 * (3 + E))

            def turn_sorted(base, m, k, group):
                wait(pe, x_sorted_in[k], 16 * group + 16)
                wait(pe, "x_staged", base + m - 1)
                pe.transpose(ps_x[k % 2][:, 0:128], x_sorted[k][:, :], ident[:, :]).then_inc(S["xs_turned"], 1)

            for base, count, _, experts in SEGMENTS:
                def weights(m):
                    if experts:
                        return pe.value_load(slot_weight_i[0:1, bass.ds(m, 1)], min_val=0, max_val=E - 1)
                    return E

                def item(m, group, k, has):
                    j = k % 2
                    if experts and has(1):
                        turn_sorted(base, m + 1, (k + 1) % DEPTH, group + (k + 1) // DEPTH)
                    if has(0):
                        e = weights(m)
                        wait(pe, "x_staged", base + m + 1)
                        wait(pe, "hid_ready", base + m - 1)
                        if experts:
                            settle(pe)
                        pe.matmul(ps_gu[j], x_stage[j][:, :], w_gu[:, bass.ds(e * 2 * FF, 2 * FF)],
                                  start=True, stop=True).then_inc(S["gu_done"], 1)
                    if has(-1):
                        wait(pe, "hid_ready", base + m)
                        for c in range(FC):
                            last = pe.transpose(ps_ht[1 - j][:, c * 128:(c + 1) * 128], hid[1 - j][:, c * 128:(c + 1) * 128], ident[:, :])
                        last.then_inc(S["hid_turned"], 1)
                    if has(-2):
                        e = weights(m - 2)
                        wait(pe, "hid_t_ready", base + m - 1)
                        wait(pe, "y_kept", base + m - 3 if type(m) is not int or m > 2 else base)
                        if experts:
                            settle(pe)
                        for c in range(FC):
                            last = pe.matmul(ps_y[j][:, 0:D], hid_t[j][:, c, :], w_down[:, bass.ds((e * FC + c) * D, D)],
                                             start=(c == 0), stop=(c == FC - 1))
                        last.then_inc(S["down_done"], 1)

                if experts:
                    pe.wait_ge(S["table_ready"], 3)
                    turn_sorted(base, 0, 0, 0)
                over_items(pe, count, item)


def kernel(**inputs):
    import numpy as np
    import concourse.bacc as bacc
    from concourse.bass_utils import run_bass_kernel_spmd as run

    g = {k: np.asarray(v) for k, v in inputs.items()}
    ctx = g["ctx_1024"]
    B, NK, D = ctx.shape
    full = NK // 128 * 128
    arrays = {
        "x": g["x"],
        "ctx_t": ctx.transpose(0, 2, 1),
        "ctx_n": ctx[:, :full].reshape(B, full // 128, 128, D).transpose(0, 2, 1, 3),
        "ctx_tail": ctx[:, full:],
        "gates": np.concatenate([g["g_xattn"], g["g_ffn"]]),
        "wq": g["L0_xattn_Wq"], "wk": g["L0_xattn_Wk"], "wv": g["L0_xattn_Wv"], "wo_t": g["L0_xattn_Wo"].T,
        "bq": g["L0_xattn_bq"], "bv": g["L0_xattn_bv"], "bo": g["L0_xattn_bo"],
        "router_t": g["L0_ffn_router_w"].T,
        "expert_gu": np.concatenate([g["L0_ffn_expert_gate"], g["L0_ffn_expert_up"]], axis=2).transpose(1, 0, 2),
        "expert_down": g["L0_ffn_expert_down"],
        "shared_gu": np.concatenate([g["L0_ffn_shared_gate"], g["L0_ffn_shared_up"]], axis=1),
        "shared_down": g["L0_ffn_shared_down"],
    }
    arrays = {k: np.ascontiguousarray(v) for k, v in arrays.items()}
    nc = bacc.Bacc("TRN2", target_bir_lowering=False, num_devices=1)
    args = [nc.dram_tensor(k, v.shape, mybir.dt.from_np(v.dtype), kind="ExternalInput").ap() for k, v in arrays.items()]
    out = nc.dram_tensor("out", g["x"].shape, F32, kind="ExternalOutput").ap()
    flamingo_layer(nc, *args, out)
    return run(nc, [arrays], core_ids=[0]).results[0]["out"]
```

```python
import concourse.bass as bass
from concourse import mybir
from contextlib import ExitStack

F32 = mybir.dt.float32
F32R = mybir.dt.float32r
BF16 = mybir.dt.bfloat16
I32 = mybir.dt.int32
U32 = mybir.dt.uint32
ALU = mybir.AluOpType
ACT = mybir.ActivationFunctionType
AX = mybir.AxisListType


def flamingo_layer(nc, x, ctx_t, ctx_n, ctx_tail, weights, bias_row, expert_gu, expert_down, shared_gu, shared_down, out):
    B, D, NK = ctx_t.shape
    T = x.shape[1] // 128
    NT = B * T
    E = expert_down.shape[0]
    FF = expert_down.shape[1]
    FC = FF // 128
    BANK = 512
    KC = -(-NK // 128)
    KF = NK // 128
    KR = NK - KF * 128
    SB = -(-NK // BANK)
    NKP = NK + NK % 2
    HALF = KC // 2 * 128
    SCALE = float(D) ** -0.5
    EPS = 1e-5
    REGION = NT + 1
    NJ = NT + E - 1
    SPARE = NJ - NT
    EMPTY = E + SPARE
    ROWS = (E * REGION + SPARE) * 128
    SLOTS = -(-NJ // 4) * 4
    EARLY = 18
    RETURN = 8
    ADDED = B // 2 - 1
    WARM = 8
    DEPTH = 4
    assert EARLY <= NT - T and RETURN + ADDED <= NT - EARLY + 2
    assert 4 * 128 <= HALF and HALF - BANK >= 256 and NK - HALF <= 2 * BANK
    assert D == 128 and T == 2 and SB == 4 and KC - KF == 1 and B % 2 == 0 and B >= E + 6 and E % 2 == 0 and FC == 2 and EARLY % 2 == 0

    sorted_x = nc.dram_tensor("sorted_x", (ROWS, D + 1), F32).ap()
    token_y = nc.dram_tensor("token_y", ((NT + EMPTY) * 128, D), F32).ap()

    ctx = ExitStack()
    with ctx:
        def sb(name, shape, dt=F32):
            return ctx.enter_context(nc.sbuf_tensor(name, shape, dt))

        def pb(name, shape, dt=F32):
            return ctx.enter_context(nc.psum_tensor(name, shape, dt))

        X = sb("X", [128, B, T, D])
        ctx_raw = [sb(f"ctx_raw{i}", [128, NKP]) for i in range(2)]
        ctx_hi = [sb(f"ctx_hi{i}", [128, NKP], F32R) for i in range(2)]
        ctx_lo = [sb(f"ctx_lo{i}", [128, NKP], F32R) for i in range(2)]
        ctx_rows_all = sb("ctx_rows_all", [128, 2 * KC * D])
        ctx_rows = [ctx_rows_all[:, i * KC * D:(i + 1) * KC * D].rearrange("p (c d) -> p c d", d=D) for i in range(2)]
        probs = [sb(f"probs{i}", [128, NK]) for i in range(T)]
        probs_t_all = sb("probs_t_all", [128, 2 * KC * T * 128])
        probs_t = [probs_t_all[:, i * KC * T * 128:(i + 1) * KC * T * 128].rearrange("p (c t q) -> p c t q", t=T, q=128)
                   for i in range(2)]
        y_token = probs_t_all[:, 0:NT * D].rearrange("p (n d) -> p n d", d=D)
        q_hi = [sb(f"q_hi{i}", [128, T * 128], F32R) for i in range(2)]
        q_lo = [sb(f"q_lo{i}", [128, T * 128], F32R) for i in range(2)]
        xn = sb("xn", [128, T, D])
        xn_t = sb("xn_t", [128, T * 128])
        o_t = sb("o_t", [128, T * 128])
        w_in = sb("w_in", [128, 4 * D + E + 2])
        w_q, w_k, w_v, w_o = (w_in[:, n * D:(n + 1) * D] for n in range(4))
        w_router = w_in[:, 4 * D:4 * D + E]
        b_q, b_v = (w_in[:, 4 * D + E + n:4 * D + E + n + 1] for n in range(2))
        row_in = sb("row_in", [128, D + 2])
        m_qk = sb("m_qk", [128, D])
        c_qk = sb("c_qk", [128, 1])
        w_vo = sb("w_vo", [128, D])
        b_vo = sb("b_vo", [128, D])
        b_v_cols = o_t[:, 0:128]
        g_tanh = sb("g_tanh", [128, 2])
        ident = sb("ident", [128, 128])
        ones = sb("ones", [128, 128], BF16)
        empty = sb("empty", [128, EMPTY, D + 1])
        before = sb("before", [128, 128], BF16)
        powers = sb("powers", [128, 2, T])
        stats = sb("stats", [128, T, 6])
        mv = sb("mv", [128, 2, T, 2])
        rstd = sb("rstd", [128, 2, T])
        stats2 = sb("stats2", [128, T, 6])
        mv2 = sb("mv2", [128, 2, T, 2])
        rstd2 = sb("rstd2", [128, 2, T])
        mx = sb("mx", [128, 2, 2])
        neg_max = sb("neg_max", [128, 2])
        den = sb("den", [128, 2, T, 2])
        den_sum = sb("den_sum", [128, T])
        den_inv = sb("den_inv", [128, T])
        xn2 = [sb(f"xn2_{i}", [128, T, D]) for i in range(2)]
        xn2_new = sb("xn2_new", [128, T * 128])
        xn2_hi = sb("xn2_hi", [128, NT, 128], F32R)
        xn2_lo = sb("xn2_lo", [128, NT, 128], F32R)
        rank_i = sb("rank_i", [128, T, E], I32)
        rank_f = sb("rank_f", [128, T, E])
        region_i = sb("region_i", [128, T, E], I32)
        region_f = sb("region_f", [128, T, E])
        top = sb("top", [128, 2, T])
        tie = sb("tie", [128, T, E])
        first = sb("first", [128, T])
        onehot = sb("onehot", [128, 2, T, E], BF16)
        seen = sb("seen", [128, T, E], BF16)
        place = sb("place", [128, T, E])
        row_f = sb("row_f", [128, T])
        row_new = [sb(f"row_new{i}", [128, T], U32) for i in range(2)]
        e_top = sb("e_top", [128, 2, T])
        score = sb("score", [128, T])
        xs = [sb(f"xs{i}", [128, T, D + 1]) for i in range(2)]
        number_i = sb("number_i", [128, 2 * T], I32)
        empty_i = sb("empty_i", [128, EMPTY], I32)
        count_f = sb("count_f", [128, E])
        count_i = sb("count_i", [128, E], I32)
        tiles = sb("tiles", [128, E])
        tiles_end = sb("tiles_end", [128, E])
        up_to = sb("up_to", [128, E, E])
        up_to_tiles = sb("up_to_tiles", [128, E, E])
        slot_i = sb("slot_i", [128, SLOTS, 1], I32)
        slot_f = sb("slot_f", [128, SLOTS, 1])
        past = sb("past", [128, SLOTS, E])
        slot_expert = sb("slot_expert", [128, SLOTS])
        slot_base = sb("slot_base", [128, SLOTS])
        slot_tile = sb("slot_tile", [128, SLOTS])
        slot_tile_i = sb("slot_tile_i", [128, SLOTS], I32)
        slot_weight_i = sb("slot_weight_i", [128, SLOTS], I32)
        w_gu_hi = sb("w_gu_hi", [128, 2 * FF * (E + 1)], F32R)
        w_gu_lo = sb("w_gu_lo", [128, 2 * FF * (E + 1)], F32R)
        w_raw = [sb(f"w_raw{i}", [128, 2 * FF]) for i in range(2)]
        w_down_shared = sb("w_down_shared", [128, FC * D])
        w_down = ctx_rows_all[:, 0:E * FC * D]
        x_sorted = [probs[1][:, i * (D + 1):(i + 1) * (D + 1)] for i in range(DEPTH)]
        y_sorted = [probs[0][:, i * D:(i + 1) * D] for i in range(DEPTH)]
        numbers = sb("numbers", [128, SLOTS], U32)
        number_out = [sb(f"number_out{i}", [128, 1], U32) for i in range(DEPTH)]
        x_hi = [ctx_hi[0][:, i * 128:(i + 1) * 128] for i in range(2)]
        x_lo = [ctx_lo[0][:, i * 128:(i + 1) * 128] for i in range(2)]
        silu = [ctx_raw[0][:, i * FF:(i + 1) * FF] for i in range(2)]
        hid = [ctx_raw[0][:, (2 + i) * FF:(3 + i) * FF] for i in range(2)]
        hid_t = [ctx_raw[1][:, i * FF:(i + 1) * FF].rearrange("p (c q) -> p c q", c=FC) for i in range(2)]

        ps_s = pb("ps_s", [128, SB * BANK])
        ps_t = [pb(f"ps_t{i}", [128, BANK]) for i in range(2)]
        ps_o = pb("ps_o", [128, BANK])
        ps_q = pb("ps_q", [128, BANK])
        ps_place = ps_q[:, 256:256 + T * E].rearrange("p (t e) -> p t e", e=E)
        ps_logit = ps_q[:, 256 + T * E:256 + 2 * T * E].rearrange("p (t e) -> p t e", e=E)
        ps_count = ps_q[:, 256 + 2 * T * E:256 + 2 * T * E + E]
        ps_gu = [ps_s[:, 0:BANK], ps_s[:, BANK:2 * BANK]]
        ps_ht = [ps_s[:, 2 * BANK:3 * BANK], ps_s[:, 3 * BANK:4 * BANK]]
        ps_y = ps_t
        ps_x = [ps_q, ps_o]

        names = ("ld_x ld_x_rest ld_w ld_ffn pads_stored more_pads_stored zeros_stored "
                 "settled const_ready matrix_ready pad_ready gates_ready bias_cols fold_done fold_ready "
                 "scores_done max_part neg_max_ready exp_done turned_done pt_act pt_dve "
                 "stats_part stats_ready veps_ready rstd_ready xn_ready xt_done xt_ready "
                 "query_done q_hi_ready q_lo_ready ctx_hi_ready ctx_lo_ready pv_done o_ready proj_done "
                 "den_part den_ready x_bias_ready x2_ready stats2_part stats2_ready "
                 "veps2_ready rstd2_ready xn2_ready xn2_turned xn2_new_ready xn2_hi_ready logits_done "
                 "rank_ready top_ready route_step onehot_ready seen_step seen_ready places_done place_step row_ready numbered numbers_kept number_ready returned "
                 "e_top_ready score_part score_ready xs_ready counted table_step table_ready "
                 "xn2_lo_ready w_down_in w_gu_in w_hi_ready w_lo_ready x_hi_ready x_lo_ready xs_turned gu_done silu_ready hid_ready hid_turned hid_t_ready down_done y_kept out_ready stored").split()
        S = {n: ctx.enter_context(nc.semaphore(n)) for n in names}

        def ring(name, n):
            return [ctx.enter_context(nc.semaphore(f"{name}{i}")) for i in range(n)]

        ctx_t_in = ring("ctx_t_in", 2)
        ctx_n_in = ring("ctx_n_in", 2)
        scattered = ring("scattered", 2)
        x_sorted_in = ring("x_sorted_in", DEPTH)
        y_out = ring("y_out", DEPTH)

        block = ctx.enter_context(nc.Block())

        def wait(eng, name, count):
            if type(count) is int and count <= 0:
                return
            eng.wait_ge(S[name] if type(name) is str else name, count)

        def settle(eng):
            eng.sem_inc(S["settled"], 1)

        def over_batches(eng, step, behind):
            def alone(b):
                step(b, b // 2, b % 2, lambda k: 0 <= b + k < B)

            for b in range(5):
                alone(b)
            with eng.Fori(2, 2 + E // 2) as i:
                step(2 * i + 1, i, 1, lambda k: True)
                step(2 * i + 2, i + 1, 0, lambda k: True)
            for b in range(5 + E, B + behind):
                alone(b)

        SEGMENTS = [(0, EARLY, 0, False), (EARLY, NJ, 0, True), (EARLY + NJ, NT - EARLY, EARLY, False)]

        def starting(b):
            return type(b) is int and b == 0

        def splits(b):
            return type(b) is not int or b == 4

        def over_items(eng, base, count, step):
            def alone(m):
                step(m, m // DEPTH, m % DEPTH, lambda k: 0 <= m + k < count)

            first = 2 if base else 4
            looped = max(0, (count - 2) // DEPTH - first) // 2 * 2
            for m in range(first * DEPTH):
                alone(m)
            if looped:
                with eng.Fori(first // 2, (first + looped) // 2) as i:
                    for g in range(2):
                        for k in range(DEPTH):
                            step(2 * DEPTH * i + DEPTH * g + k, 2 * i + g, k, lambda n: True)
            for m in range(DEPTH * (first + looped), count + 2):
                alone(m)

        def close_region(eng, e, done):
            n = eng.value_load(count_i[0:1, e:e + 1], min_val=0, max_val=NT * 128)
            eng.dma_start(sorted_x[bass.ds(n + e * REGION * 128, 128), :], empty[:, e, :]).then_inc(S[done], 16)

        @block.sync
        def _(sp):
            sp.dma_start(X[:, 0:2, :, :], x[0:2].rearrange("b (p t) d -> p b t d", t=T)).then_inc(S["ld_x"], 16)
            sp.dma_start(ctx_raw[0][:, 0:NK], ctx_t[0]).then_inc(ctx_t_in[0], 16)
            sp.dma_start(w_in[:, :], weights).then_inc(S["ld_w"], 16)
            sp.dma_start(row_in[:, :], bias_row.rearrange("(o d) -> o d", o=1).to_broadcast([128, D + 2])).then_inc(S["ld_w"], 16)

            def load_rows(b, par):
                sp.dma_start(ctx_rows[par][:, 0:KF, :], ctx_n[b]).then_inc(ctx_n_in[par], 16)
                sp.dma_start(ctx_rows[par][0:KR, KF, :], ctx_tail[b]).then_inc(ctx_n_in[par], 16)

            sp.dma_start(ctx_raw[1][:, 0:NK], ctx_t[1]).then_inc(ctx_t_in[1], 16)
            load_rows(0, 0)
            sp.dma_start(X[:, 2:B, :, :], x[2:B].rearrange("b (p t) d -> p b t d", t=T)).then_inc(S["ld_x_rest"], 16)
            load_rows(1, 1)
            sp.wait_ge(S["numbered"], 4)
            sp.dma_start(sorted_x[E * REGION * 128:, :].rearrange("(n p) d -> p n d", p=128),
                         empty[:, E:, :]).then_inc(S["zeros_stored"], 16)

            def load_context(b, par):
                wait(sp, "ctx_lo_ready", b - 1)
                settle(sp)
                sp.dma_start(ctx_raw[par][:, 0:NK], ctx_t[b]).then_inc(ctx_t_in[par], 16)
                wait(sp, "pv_done", b - 1)
                settle(sp)
                load_rows(b, par)

            for b in range(2, 4):
                load_context(b, b % 2)
            load_context(4, 0)
            sp.dma_start(w_raw[0][:, :], shared_gu).then_inc(S["w_gu_in"], 16)
            sp.dma_start(w_down_shared[:, :].rearrange("f (c d) -> f c d", c=FC),
                         shared_down.rearrange("(c f) d -> f c d", c=FC)).then_inc(S["ld_ffn"], 16)
            with sp.Fori(0, E // 2) as i:
                for k in range(2):
                    e = 2 * i + k
                    load_context(e + 5, 1 - k)
                    wait(sp, "w_gu_in", 16 * e + 16)
                    settle(sp)
                    wait(sp, "w_lo_ready", e + 1)
                    settle(sp)
                    sp.dma_start(w_raw[1 - k][:, :], expert_gu[:, e, :]).then_inc(S["w_gu_in"], 16)
            for b in range(5 + E, B):
                load_context(b, b % 2)
            sp.wait_ge(S["pv_done"], B)
            sp.dma_start(w_down.rearrange("f (n d) -> f n d", d=D),
                         expert_down.rearrange("e (c f) d -> f (e c) d", c=FC)).then_inc(S["w_down_in"], 16)

            sp.wait_ge(S["table_ready"], 1)
            for e in range(E // 2):
                close_region(sp, e, "pads_stored")
            sp.wait_ge(S["table_ready"], 3)
            for par in range(2):
                sp.wait_ge(scattered[par], 16 * NT // 2)
            sp.wait_ge(S["zeros_stored"], 16)
            sp.wait_ge(S["pads_stored"], 16 * E // 2)
            sp.wait_ge(S["more_pads_stored"], 16 * E // 2)

            def load_sorted(j, k):
                row = sp.value_load(slot_tile_i[0:1, bass.ds(j, 1)], min_val=0, max_val=ROWS // 128 - 1)
                sp.dma_start(x_sorted[k][:, :], sorted_x[bass.ds(row * 128, 128), :]).then_inc(x_sorted_in[k], 16)

            for j in range(DEPTH):
                load_sorted(j, j)

            def load_next(j, k):
                wait(sp, "numbers_kept", j + 1)
                settle(sp)
                load_sorted(j + DEPTH, k)

            looped = (NJ - DEPTH) // DEPTH
            with sp.Fori(0, looped) as i:
                for k in range(DEPTH):
                    load_next(DEPTH * i + k, k)
            for j in range(DEPTH * looped, NJ - DEPTH):
                load_next(j, j % DEPTH)

            for k in range(DEPTH):
                sp.wait_ge(y_out[k], 16 * len(range(k, NJ, DEPTH)))
            sp.dma_start(y_token[:, :, :], token_y[0:NT * 128, :].rearrange("(p n) d -> p n d", n=NT)).then_inc(S["returned"], 16)

            out_v = out.rearrange("b (p t) d -> b p t d", t=T)
            with sp.Fori(0, B // 2) as i:
                wait(sp, "out_ready", i + 1)
                sp.dma_start(out_v[bass.ds(2 * i, 2)].rearrange("b p t d -> p b t d"), X[:, bass.ds(2 * i, 2), :, :]).then_inc(S["stored"], 16)
            sp.wait_ge(S["stored"], 16 * B // 2)

        @block.gpsimd
        def _(pool):
            pool.memset(ident[:, :], 0.0).then_inc(S["const_ready"], 1)
            pool.memset(ones[:, :], 1.0).then_inc(S["const_ready"], 1)
            pool.memset(before[:, :], 1.0).then_inc(S["const_ready"], 1)
            pool.memset(powers[:, 0, :], -0.5).then_inc(S["const_ready"], 1)
            pool.memset(powers[:, 1, :], -1.0).then_inc(S["const_ready"], 1)
            pool.iota(rank_i[:, :, :], pattern=[[0, T], [-1, E]], base=E, channel_multiplier=0).then_inc(S["const_ready"], 1)
            pool.iota(slot_i[:, :, :], pattern=[[1, SLOTS], [0, 1]], base=0, channel_multiplier=0).then_inc(S["const_ready"], 1)
            pool.iota(region_i[:, :, :], pattern=[[0, T], [REGION * 128, E]], base=0, channel_multiplier=0).then_inc(S["matrix_ready"], 1)
            pool.iota(number_i[:, :], pattern=[[1, 2 * T]], base=0, channel_multiplier=NT).then_inc(S["const_ready"], 1)
            pool.iota(empty_i[:, :], pattern=[[128, EMPTY]], base=NT * 128, channel_multiplier=1).then_inc(S["const_ready"], 1)
            pool.wait_ge(S["const_ready"], 9)
            pool.affine_select(out=ident[:, :], in_=ident[:, :], compare_op=ALU.not_equal, fill=1.0, base=0,
                               pattern=[[-1, 128]], channel_multiplier=1).then_inc(S["matrix_ready"], 1)
            pool.affine_select(out=before[:, :], in_=before[:, :], compare_op=ALU.is_gt, fill=0.0, base=0,
                               pattern=[[1, 128]], channel_multiplier=-1).then_inc(S["matrix_ready"], 1)

            pool.sem_inc(S["w_lo_ready"], 1)

            def number_rows():
                pool.memset(empty[:, :, 0:D], 0.0).then_inc(S["numbered"], 1)
                for i in range(2):
                    pool.tensor_copy(xs[i][:, :, D:D + 1].rearrange("p t o -> p (t o)"),
                                     number_i[:, i * T:(i + 1) * T]).then_inc(S["numbered"], 1)
                pool.tensor_copy(empty[:, :, D:D + 1].rearrange("p n o -> p (n o)"), empty_i[:, :]).then_inc(S["numbered"], 1)

            def reciprocal_std(b, par):
                wait(pool, "stats_ready", b + 1)
                settle(pool)
                pool.tensor_scalar(mv[:, par, :, 1], mv[:, par, :, 1], EPS, None, ALU.add).then_inc(S["veps_ready"], 1)
                wait(pool, "veps_ready", b + 1)
                pool.tensor_tensor(rstd[:, par, :], mv[:, par, :, 1], powers[:, 0, :], ALU.pow).then_inc(S["rstd_ready"], 1)

            def reciprocal_std2(b, par):
                wait(pool, "stats2_ready", b + 1)
                settle(pool)
                pool.tensor_scalar(mv2[:, par, :, 1], mv2[:, par, :, 1], EPS, None, ALU.add).then_inc(S["veps2_ready"], 1)
                wait(pool, "veps2_ready", b + 1)
                pool.tensor_tensor(rstd2[:, par, :], mv2[:, par, :, 1], powers[:, 0, :], ALU.pow).then_inc(S["rstd2_ready"], 1)

            def low_part(b, par):
                wait(pool, "ctx_hi_ready", b + 1)
                pool.tensor_tensor(ctx_lo[par][:, 0:NK], ctx_raw[par][:, 0:NK], ctx_hi[par][:, 0:NK].bitcast(F32),
                                   ALU.subtract).then_inc(S["ctx_lo_ready"], 1)

            def split_low(n, par, e):
                cols = bass.ds(e * 2 * FF, 2 * FF)
                wait(pool, "w_hi_ready", n + 1)
                settle(pool)
                pool.tensor_tensor(w_gu_lo[:, cols], w_raw[par][:, :], w_gu_hi[:, cols].bitcast(F32),
                                   ALU.subtract).then_inc(S["w_lo_ready"], 1)

            def add_bias(b):
                wait(pool, "xn_ready", b + 1)
                settle(pool)
                pool.tensor_tensor(X[:, b, :, :], X[:, b, :, :],
                                   b_vo[:, :].rearrange("p (o d) -> p o d", o=1).to_broadcast([128, T, D]),
                                   ALU.add).then_inc(S["x_bias_ready"], 1)

            def scatter(b, half, par):
                wait(pool, "e_top_ready", b + 1)
                settle(pool)
                pool.tensor_scalar(e_top[:, par, :], e_top[:, par, :], 1.0, None, ALU.add).then_inc(S["score_part"], 1)
                wait(pool, "score_part", b + 1)
                pool.tensor_tensor(score[:, :], e_top[:, par, :], powers[:, 1, :], ALU.pow).then_inc(S["score_ready"], 1)
                wait(pool, "score_ready", b + 1)
                wait(pool, scattered[par], 16 * T * half)
                if type(b) is not int or b >= 2:
                    wait(pool, "numbered", b + 2)
                    settle(pool)
                    pool.tensor_scalar(xs[par][:, :, D:D + 1], xs[par][:, :, D:D + 1], float(2 * T), None,
                                       ALU.add).then_inc(S["numbered"], 1)
                pool.tensor_tensor(xs[par][:, :, 0:D], xn2[par][:, :, :],
                                   score[:, :].rearrange("p (t o) -> p t o", o=1).to_broadcast([128, T, D]),
                                   ALU.mult).then_inc(S["xs_ready"], 1)
                wait(pool, "row_ready", b + 1)
                wait(pool, "xs_ready", b + 1)
                wait(pool, "numbered", b + 3)
                settle(pool)
                for t in range(T):
                    pool.indirect_dma_start(sorted_x[:, :], bass.IndirectOffsetOnAxis(row_new[par][:, t:t + 1], 0),
                                            xs[par][:, t, :], None).then_inc(scattered[par], 16)

            def step(b, half, par, has):
                if has(-2):
                    reciprocal_std2(b - 2, par)
                if has(1) and not starting(b):
                    reciprocal_std(b + 1, 1 - par)
                    low_part(b + 1, 1 - par)
                    add_bias(b + 1)
                if has(-3):
                    scatter(b - 3, half + (par - 3) // 2, 1 - par)
                if splits(b):
                    split_low(b - 4, par, b - 5 if type(b) is not int else E)

            reciprocal_std(0, 0)
            number_rows()
            reciprocal_std(1, 1)
            low_part(1, 1)
            pool.wait_ge(S["fold_ready"], 4)
            add_bias(0)
            add_bias(1)
            over_batches(pool, step, 3)

            pool.wait_ge(S["table_ready"], 1)
            for e in range(E // 2, E):
                close_region(pool, e, "more_pads_stored")

            def scatter_result(j, group, k):
                wait(pool, y_out[k], 16 * group)
                wait(pool, "numbers_kept", j + 1)
                settle(pool)
                pool.tensor_copy(number_out[k][:, :], numbers[:, bass.ds(j, 1)]).then_inc(S["number_ready"], 1)
                wait(pool, "number_ready", j + 1)
                wait(pool, "y_kept", EARLY + j + 1)
                settle(pool)
                pool.indirect_dma_start(token_y[:, :], bass.IndirectOffsetOnAxis(number_out[k][:, 0:1], 0),
                                        y_sorted[k][:, :], None).then_inc(y_out[k], 16)

            for j in range(DEPTH):
                scatter_result(j, 0, j)
            with pool.Fori(1, NJ // DEPTH) as i:
                for k in range(DEPTH):
                    scatter_result(DEPTH * i + k, i, k)
            for j in range(NJ // DEPTH * DEPTH, NJ):
                scatter_result(j, j // DEPTH, j % DEPTH)

        @block.scalar
        def _(act):
            def high_part(b, half, par):
                wait(act, ctx_t_in[par], 16 * half + 16)
                wait(act, "scores_done", 2 * SB * (b - 1))
                act.activation(ctx_hi[par][:, 0:NK], ctx_raw[par][:, 0:NK], ACT.Copy).then_inc(S["ctx_hi_ready"], 1)

            def keep_xn_t(b):
                wait(act, "xt_done", b + 1)
                wait(act, "query_done", b)
                act.activation(xn_t[:, :], ps_q[:, 0:T * 128], ACT.Copy).then_inc(S["xt_ready"], 1)

            def query_high(b, par):
                wait(act, "query_done", b + 1)
                wait(act, "scores_done", 2 * SB * (b - 1))
                act.activation(q_hi[par][:, :], ps_q[:, T * 128:], ACT.Identity, bias=c_qk[:, 0:1]).then_inc(S["q_hi_ready"], 1)

            def exponentials(b, par, t, parts):
                tile = T * b + t
                if 0 in parts:
                    wait(act, "neg_max_ready", tile + 1)
                    wait(act, "turned_done", 4 * (tile - 1))
                for k in parts:
                    lo, hi = ((0, HALF), (HALF, NK))[k]
                    act.activation(probs[t][:, lo:hi], ps_s[:, 2 * BANK * k:2 * BANK * k + hi - lo], ACT.Exp, bias=neg_max[:, t:t + 1],
                                   accum_out=den[:, par, t, k:k + 1]).then_inc(S["exp_done"], 1)

            def keep_turned(b, par, t, g):
                if t == 0:
                    wait(act, "pv_done", b - 1)
                wait(act, "turned_done", 4 * (T * b + t) + g + 1)
                act.activation(probs_t[par][:, 4 * g:4 * g + 4, t, :],
                               ps_t[0][:, :].rearrange("p (c q) -> p c q", c=4), ACT.Copy).then_inc(S["pt_act"], 1)

            def keep_o(b):
                wait(act, "pv_done", b + 1)
                wait(act, "proj_done", b)
                act.activation(o_t[:, :], ps_o[:, 0:T * 128], ACT.Copy).then_inc(S["o_ready"], 1)

            def keep_xn2(b):
                wait(act, "xn2_turned", b + 1)
                wait(act, "logits_done", b)
                act.activation(xn2_new[:, :], ps_q[:, 0:T * 128], ACT.Copy).then_inc(S["xn2_new_ready"], 1)
                act.activation(xn2_hi[:, bass.ds(T * b, T), :], ps_q[:, 0:T * 128].rearrange("p (t q) -> p t q", t=T),
                               ACT.Copy).then_inc(S["xn2_hi_ready"], 1)

            def exp_top(b, par):
                wait(act, "top_ready", b + 1)
                wait(act, "score_ready", b - 1)
                act.activation(e_top[:, par, :], top[:, par, :], ACT.Exp, scale=-1.0).then_inc(S["e_top_ready"], 1)

            def split_high(n, par, e):
                cols = bass.ds(e * 2 * FF, 2 * FF)
                wait(act, "w_gu_in", 16 * n + 16)
                settle(act)
                act.activation(w_gu_hi[:, cols], w_raw[par][:, :], ACT.Copy).then_inc(S["w_hi_ready"], 1)

            def step(b, half, par, has):
                if has(-1):
                    keep_turned(b - 1, 1 - par, 1, 0)
                    keep_turned(b - 1, 1 - par, 1, 2)
                if starting(b):
                    keep_xn_t(1)
                if has(0):
                    exponentials(b, par, 0, (0, 1))
                if starting(b):
                    query_high(1, 1)
                if has(-3):
                    exp_top(b - 3, 1 - par)
                if has(-2):
                    keep_xn2(b - 2)
                if has(0):
                    keep_turned(b, par, 0, 0)
                if has(1) and not starting(b):
                    high_part(b + 1, half + (par + 1) // 2, 1 - par)
                if has(0):
                    keep_turned(b, par, 0, 2)
                if has(1) and not starting(b):
                    keep_xn_t(b + 1)
                if has(0):
                    exponentials(b, par, 1, (0,))
                if has(1) and not starting(b):
                    query_high(b + 1, 1 - par)
                if has(0):
                    exponentials(b, par, 1, (1,))
                if has(-1):
                    keep_o(b - 1)
                if splits(b):
                    split_high(b - 4, par, b - 5 if type(b) is not int else E)

            act.wait_ge(S["pad_ready"], 5)
            high_part(0, 0, 0)
            act.wait_ge(S["ld_w"], 16 * 2)
            act.activation(g_tanh[:, :], row_in[:, D:D + 2], ACT.Tanh).then_inc(S["gates_ready"], 1)
            keep_xn_t(0)
            act.wait_ge(S["fold_ready"], 2)
            query_high(0, 0)
            high_part(1, 0, 1)
            over_batches(act, step, 1)
            exp_top(B - 2, 0)

            def finish(m):
                if m == 4:
                    keep_xn2(B - 1)
                elif m == 7:
                    exp_top(B - 1, 1)

            for base, count, tile0, experts in SEGMENTS:
                def stage_high(m, j):
                    if type(m) is not int or m > 1:
                        wait(act, "gu_done", base + m - 1)
                    wait(act, "xs_turned", m + 1)
                    settle(act)
                    act.activation(x_hi[j][:, :], ps_x[j][:, 0:128], ACT.Copy).then_inc(S["x_hi_ready"], 1)

                if experts:
                    for m in range(2):
                        stage_high(m, m)

                def item(m, group, k, has):
                    j = k % 2
                    if has(0):
                        wait(act, "gu_done", base + m + 1)
                        act.activation(silu[j][:, :], ps_gu[j][:, 0:FF], ACT.Silu).then_inc(S["silu_ready"], 1)
                    if has(-1):
                        wait(act, "hid_turned", base + m)
                        act.activation(hid_t[1 - j][:, :, :], ps_ht[1 - j][:, 0:FF].rearrange("p (c q) -> p c q", c=FC),
                                       ACT.Copy).then_inc(S["hid_t_ready"], 1)
                    if experts and has(2):
                        stage_high(m + 2, j)
                    if base == 0 and type(m) is int:
                        finish(m)

                over_items(act, base, count, item)

        @block.vector
        def _(dve):
            for i in range(2):
                dve.memset(ctx_hi[i][:, NK:NKP].bitcast(F32), 0.0).then_inc(S["pad_ready"], 1)
                dve.memset(ctx_lo[i][:, NK:NKP].bitcast(F32), 0.0).then_inc(S["pad_ready"], 1)
            dve.memset(seen[:, :, :], 0.0).then_inc(S["pad_ready"], 1)

            def statistics(b, par):
                wait(dve, "stats_ready", b)
                settle(dve)
                for t in range(T):
                    last = dve.bn_stats(stats[:, t, :], X[:, b, t, :])
                last.then_inc(S["stats_part"], 1)
                wait(dve, "stats_part", b + 1)
                wait(dve, "xn_ready", b - 1)
                settle(dve)
                for t in range(T):
                    last = dve.bn_aggr(mv[:, par, t, :], stats[:, t, :])
                last.then_inc(S["stats_ready"], 1)

            def normalize(b, par):
                wait(dve, "rstd_ready", b + 1)
                wait(dve, "xt_done", b)
                for t in range(T):
                    last = dve.tensor_scalar(xn[:, t, :], X[:, b, t, :], mv[:, par, t, 0:1], rstd[:, par, t:t + 1],
                                             ALU.subtract, ALU.mult)
                last.then_inc(S["xn_ready"], 1)

            def keep_xn2_lo(b):
                wait(dve, "xn2_hi_ready", b + 1)
                settle(dve)
                dve.tensor_tensor(xn2_lo[:, bass.ds(T * b, T), :], xn2_new[:, :].rearrange("p (t q) -> p t q", t=T),
                                  xn2_hi[:, bass.ds(T * b, T), :].bitcast(F32), ALU.subtract).then_inc(S["xn2_lo_ready"], 1)

            def part_max(b, t, k):
                tile = T * b + t
                lo, hi = ((0, HALF), (HALF, NK))[k]
                wait(dve, "scores_done", SB * tile + 2 * k + 2)
                dve.tensor_reduce(mx[:, t, k:k + 1], ps_s[:, 2 * BANK * k:2 * BANK * k + hi - lo], AX.X, ALU.max, negate=True).then_inc(S["max_part"], 1)
                if k == 1:
                    wait(dve, "max_part", 2 * tile + 2)
                    dve.tensor_tensor(neg_max[:, t:t + 1], mx[:, t, 0:1], mx[:, t, 1:2], ALU.min).then_inc(S["neg_max_ready"], 1)

            def keep_turned(b, par, t, g):
                if t == 0:
                    wait(dve, "pv_done", b - 1)
                wait(dve, "turned_done", 4 * (T * b + t) + g + 1)
                if g == 1:
                    dve.tensor_copy(probs_t[par][:, 4:8, t, :], ps_t[1][:, :].rearrange("p (c q) -> p c q", c=4)).then_inc(S["pt_dve"], 1)
                else:
                    dve.tensor_copy(probs_t[par][0:KR, KF, t, :], ps_t[1][0:KR, 0:128]).then_inc(S["pt_dve"], 1)

            def query_low(b, par):
                wait(dve, "q_hi_ready", b + 1)
                dve.scalar_tensor_tensor(out=q_lo[par][:, :], in0=ps_q[:, T * 128:], scalar=c_qk[:, 0:1],
                                         in1=q_hi[par][:, :].bitcast(F32), op0=ALU.add, op1=ALU.subtract).then_inc(S["q_lo_ready"], 1)

            def result(b, par):
                wait(dve, "exp_done", 2 * T * b + 2 * T)
                wait(dve, "x2_ready", b)
                dve.tensor_tensor(den_sum[:, :], den[:, par, :, 0], den[:, par, :, 1], ALU.add).then_inc(S["den_part"], 1)
                wait(dve, "den_part", b + 1)
                dve.reciprocal(den_inv[:, :], den_sum[:, :]).then_inc(S["den_ready"], 1)
                wait(dve, "den_ready", b + 1)
                wait(dve, "proj_done", b + 1)
                wait(dve, "x_bias_ready", b + 1)
                for t in range(T):
                    last = dve.scalar_tensor_tensor(out=X[:, b, t, :], in0=ps_o[:, (T + t) * 128:(T + t + 1) * 128],
                                                    scalar=den_inv[:, t:t + 1], in1=X[:, b, t, :], op0=ALU.mult, op1=ALU.add)
                last.then_inc(S["x2_ready"], 1)

            def statistics2(b, par):
                wait(dve, "x2_ready", b + 1)
                wait(dve, "stats2_ready", b)
                settle(dve)
                for t in range(T):
                    last = dve.bn_stats(stats2[:, t, :], X[:, b, t, :])
                last.then_inc(S["stats2_part"], 1)
                wait(dve, "stats2_part", b + 1)
                wait(dve, "xn2_ready", b - 1)
                settle(dve)
                for t in range(T):
                    last = dve.bn_aggr(mv2[:, par, t, :], stats2[:, t, :])
                last.then_inc(S["stats2_ready"], 1)

            def normalize2(b, par):
                wait(dve, "rstd2_ready", b + 1)
                wait(dve, "xn2_turned", b - 1)
                wait(dve, "xs_ready", b - 1)
                for t in range(T):
                    last = dve.tensor_scalar(xn2[par][:, t, :], X[:, b, t, :], mv2[:, par, t, 0:1], rstd2[:, par, t:t + 1],
                                             ALU.subtract, ALU.mult)
                last.then_inc(S["xn2_ready"], 1)

            def bcast(v):
                return v.rearrange("p (t o) -> p t o", o=1).to_broadcast([128, T, E])

            def find_top(b, par):
                wait(dve, "logits_done", b + 1)
                wait(dve, "e_top_ready", b - 1)
                dve.tensor_reduce(top[:, par, :], ps_logit, AX.X, ALU.max).then_inc(S["top_ready"], 1)
                wait(dve, "top_ready", b + 1)
                wait(dve, "route_step", 3 * b)
                dve.tensor_tensor(tie[:, :, :], ps_logit, bcast(top[:, par, :]), ALU.is_equal).then_inc(S["route_step"], 1)

            def choose(b, par):
                wait(dve, "route_step", 3 * b + 1)
                dve.tensor_tensor(tie[:, :, :], tie[:, :, :], rank_f[:, :, :], ALU.mult).then_inc(S["route_step"], 1)
                wait(dve, "route_step", 3 * b + 2)
                dve.tensor_reduce(first[:, :], tie[:, :, :], AX.X, ALU.max).then_inc(S["route_step"], 1)
                wait(dve, "route_step", 3 * b + 3)
                dve.tensor_tensor(onehot[:, par, :, :], tie[:, :, :], bcast(first[:, :]), ALU.is_equal).then_inc(S["onehot_ready"], 1)
                wait(dve, "onehot_ready", b + 1)
                wait(dve, "seen_step", b)
                dve.tensor_tensor(seen[:, 1, :], seen[:, 0, :], onehot[:, par, 0, :], ALU.add).then_inc(S["seen_ready"], 1)

            def add_region(b):
                wait(dve, "places_done", b + 1)
                wait(dve, "xn2_hi_ready", b + 2 if type(b) is not int or b < B - 2 else b + 1)
                dve.tensor_tensor(place[:, :, :], ps_place, region_f[:, :, :], ALU.add).then_inc(S["place_step"], 1)

            def find_place(b, half, par):
                wait(dve, "place_step", 3 * b + 1)
                dve.tensor_tensor(place[:, :, :], place[:, :, :], onehot[:, par, :, :], ALU.mult).then_inc(S["place_step"], 1)
                wait(dve, "place_step", 3 * b + 2)
                dve.tensor_reduce(row_f[:, :], place[:, :, :], AX.X, ALU.add).then_inc(S["place_step"], 1)
                wait(dve, "place_step", 3 * b + 3)
                wait(dve, scattered[par], 16 * T * half)
                dve.tensor_copy(row_new[par][:, :], row_f[:, :]).then_inc(S["row_ready"], 1)
                dve.tensor_tensor(seen[:, 0, :], seen[:, 1, :], onehot[:, par, 1, :], ALU.add).then_inc(S["seen_step"], 1)
                wait(dve, "row_ready", b + 1)
                settle(dve)

            def step(b, half, par, has):
                if has(-2):
                    result(b - 2, par)
                    statistics2(b - 2, par)
                if has(0):
                    part_max(b, 0, 0)
                if has(-1):
                    keep_turned(b - 1, 1 - par, 1, 1)
                if has(0):
                    part_max(b, 0, 1)
                if has(-2):
                    normalize2(b - 2, par)
                if type(b) is int and b == 1:
                    dve.wait_ge(S["ld_x_rest"], 16)
                if starting(b):
                    query_low(1, 1)
                elif has(1):
                    statistics(b + 1, 1 - par)
                if has(-1):
                    keep_turned(b - 1, 1 - par, 1, 3)
                if has(1) and not starting(b):
                    normalize(b + 1, 1 - par)
                if has(-3):
                    add_region(b - 3)
                if has(0):
                    part_max(b, 1, 0)
                    keep_turned(b, par, 0, 1)
                if has(-2):
                    find_top(b - 2, par)
                if has(0):
                    part_max(b, 1, 1)
                    keep_turned(b, par, 0, 3)
                if has(-2):
                    keep_xn2_lo(b - 2)
                if has(-3):
                    find_place(b - 3, half + (par - 3) // 2, 1 - par)
                if has(-2):
                    choose(b - 2, par)
                if has(1) and not starting(b):
                    query_low(b + 1, 1 - par)

            dve.wait_ge(S["ld_x"], 16)
            statistics(0, 0)
            normalize(0, 0)
            dve.wait_ge(S["ld_w"], 16 * 2)
            dve.tensor_copy(b_v_cols[:, :], b_v.to_broadcast([128, 128])).then_inc(S["bias_cols"], 1)
            dve.wait_ge(S["fold_done"], 1)
            dve.tensor_scalar(m_qk[:, :], ps_o[:, 0:128], SCALE, None, ALU.mult).then_inc(S["fold_ready"], 1)
            dve.tensor_scalar(c_qk[:, :], ps_o[:, 384:385], SCALE, None, ALU.mult).then_inc(S["fold_ready"], 1)
            dve.wait_ge(S["ctx_hi_ready"], 1)
            dve.tensor_tensor(ctx_lo[0][:, 0:NK], ctx_raw[0][:, 0:NK], ctx_hi[0][:, 0:NK].bitcast(F32),
                              ALU.subtract).then_inc(S["ctx_lo_ready"], 1)
            query_low(0, 0)
            statistics(1, 1)
            dve.wait_ge(S["gates_ready"], 1)
            dve.tensor_scalar(w_vo[:, :], ps_o[:, 128:256], g_tanh[:, 0:1], None, ALU.mult).then_inc(S["fold_ready"], 1)
            dve.tensor_tensor(b_vo[:, :], ps_o[:, 256:384], row_in[:, 0:D], ALU.add).then_inc(S["bias_cols"], 1)
            dve.wait_ge(S["bias_cols"], 2)
            dve.tensor_scalar(b_vo[:, :], b_vo[:, :], g_tanh[:, 0:1], None, ALU.mult).then_inc(S["fold_ready"], 1)
            normalize(1, 1)
            dve.wait_ge(S["matrix_ready"], 3)
            dve.tensor_copy(rank_f[:, :, :], rank_i[:, :, :]).then_inc(S["rank_ready"], 1)
            dve.tensor_copy(region_f[:, :, :], region_i[:, :, :]).then_inc(S["rank_ready"], 1)
            dve.tensor_copy(slot_f[:, :, :], slot_i[:, :, :]).then_inc(S["rank_ready"], 1)
            dve.wait_ge(S["rank_ready"], 3)
            dve.tensor_tensor(up_to[:, :, :], rank_f[:, 0, :].rearrange("p (o f) -> p o f", o=1).to_broadcast([128, E, E]),
                              rank_f[:, 0, :].rearrange("p (e o) -> p e o", o=1).to_broadcast([128, E, E]),
                              ALU.is_ge).then_inc(S["rank_ready"], 1)
            dve.wait_ge(S["rank_ready"], 4)
            over_batches(dve, step, 1)

            steps = [0]

            def table(op):
                wait(dve, "table_step", steps[0])
                op().then_inc(S["table_step"], 1)
                steps[0] += 1

            def by_slot(v):
                return v.to_broadcast([128, SLOTS, E])

            def by_expert(v):
                return v.rearrange("p (o e) -> p o e", o=1).to_broadcast([128, SLOTS, E])

            def slots(v):
                return v.rearrange("p (j o) -> p j o", o=1)

            def count_tiles():
                dve.tensor_copy(count_i[:, :], ps_count).then_inc(S["table_ready"], 1)
                table(lambda: dve.tensor_copy(count_f[:, :], ps_count))
                table(lambda: dve.scalar_tensor_tensor(out=past[:, :, :], in0=by_slot(slot_f[:, :, :]), scalar=128.0,
                                                       in1=by_expert(count_f[:, :]), op0=ALU.mult, op1=ALU.is_lt))

            def sum_tiles():
                table(lambda: dve.tensor_reduce(tiles[:, :], past[:, :, :].rearrange("p j e -> p e j"), AX.X, ALU.add))
                table(lambda: dve.tensor_tensor(up_to_tiles[:, :, :], up_to[:, :, :],
                                                tiles[:, :].rearrange("p (o e) -> p o e", o=1).to_broadcast([128, E, E]), ALU.mult))
                table(lambda: dve.tensor_reduce(tiles_end[:, :], up_to_tiles[:, :, :], AX.X, ALU.add))

            def find_experts():
                table(lambda: dve.tensor_tensor(past[:, :, :], by_slot(slot_f[:, :, :]), by_expert(tiles_end[:, :]), ALU.is_ge))
                table(lambda: dve.tensor_reduce(slot_expert[:, :], past[:, :, :], AX.X, ALU.add))

            def sum_before():
                table(lambda: dve.tensor_tensor(past[:, :, :], past[:, :, :], by_expert(tiles[:, :]), ALU.mult))
                table(lambda: dve.tensor_reduce(slot_base[:, :], past[:, :, :], AX.X, ALU.add))

            def find_tiles():
                table(lambda: dve.scalar_tensor_tensor(out=slot_tile[:, :], in0=slot_expert[:, :], scalar=float(REGION),
                                                       in1=slot_base[:, :], op0=ALU.mult, op1=ALU.subtract))
                table(lambda: dve.tensor_tensor(slot_tile[:, :], slot_tile[:, :], slot_f[:, :, :].rearrange("p j o -> p (j o)"), ALU.add))
                table(lambda: dve.tensor_scalar(slot_expert[:, :], slot_expert[:, :], float(E - 1), None, ALU.min))
                dve.wait_ge(S["table_step"], steps[0])
                dve.tensor_copy(slot_tile_i[:, :], slot_tile[:, :]).then_inc(S["table_ready"], 1)
                dve.tensor_copy(slot_weight_i[:, :], slot_expert[:, :]).then_inc(S["table_ready"], 1)

            def finish(m):
                if m == 1:
                    result(B - 1, 1)
                    statistics2(B - 1, 1)
                elif m == 2:
                    add_region(B - 2)
                    find_place(B - 2, B // 2 - 1, 0)
                elif m == 3:
                    normalize2(B - 1, 1)
                elif m == 6:
                    find_top(B - 1, 1)
                    choose(B - 1, 1)
                    keep_xn2_lo(B - 1)
                elif m == 9:
                    dve.wait_ge(S["counted"], 1)
                    add_region(B - 1)
                    find_place(B - 1, B // 2 - 1, 1)
                elif m == 10:
                    count_tiles()
                elif m == 11:
                    sum_tiles()
                elif m == 12:
                    find_experts()
                elif m == 13:
                    sum_before()
                elif m == 14:
                    find_tiles()

            x_tiles = X[:, :, :, :].rearrange("p b t d -> p (b t) d")

            def stage_sorted(m, j, k):
                wait(dve, "x_hi_ready", m + 1)
                settle(dve)
                dve.tensor_tensor(x_lo[j][:, :], ps_x[j][:, 0:128], x_hi[j][:, :].bitcast(F32), ALU.subtract).then_inc(S["x_lo_ready"], 1)
                dve.tensor_copy(numbers[:, bass.ds(m, 1)], x_sorted[k][:, D:D + 1]).then_inc(S["numbers_kept"], 1)

            def add_experts(i):
                wait(dve, "returned", 16)
                wait(dve, "y_kept", NJ + 2 * T * (i + 1))
                settle(dve)
                rows = X[:, bass.ds(2 * i, 2), :, :].rearrange("p b t d -> p (b t) d")
                dve.tensor_tensor(rows, rows, y_token[:, bass.ds(2 * T * i, 2 * T), :], ALU.add).then_inc(S["out_ready"], 1)

            def feed_forward(base, count, tile0, experts, adds):
                def item(m, group, k, has):
                    j = k % 2
                    if has(0):
                        wait(dve, "silu_ready", base + m + 1)
                        dve.tensor_tensor(hid[j][:, :], ps_gu[j][:, FF:2 * FF], silu[j][:, :], ALU.mult).then_inc(S["hid_ready"], 1)
                    if experts and has(2):
                        stage_sorted(m + 2, j, (k + 2) % DEPTH)
                    if has(-2):
                        wait(dve, "down_done", base + m - 1)
                        if experts:
                            wait(dve, y_out[(k - 2) % DEPTH], 16 * (group + (k - 2) // DEPTH))
                            dve.tensor_scalar(y_sorted[(k - 2) % DEPTH][:, :], ps_y[j][:, 0:D], g_tanh[:, 1:2], None,
                                              ALU.mult).then_inc(S["y_kept"], 1)
                        else:
                            settle(dve)
                            dve.scalar_tensor_tensor(out=x_tiles[:, tile0 + m - 2, :], in0=ps_y[j][:, 0:D], scalar=g_tanh[:, 1:2],
                                                     in1=x_tiles[:, tile0 + m - 2, :], op0=ALU.mult,
                                                     op1=ALU.add).then_inc(S["y_kept"], 1)
                    if base == 0 and type(m) is int:
                        finish(m)
                    if adds and (type(m) is not int or RETURN <= m < RETURN + ADDED):
                        add_experts(m - RETURN)

                if experts:
                    for m in range(2):
                        stage_sorted(m, m, m)
                over_items(dve, base, count, item)

            feed_forward(*SEGMENTS[0], False)
            feed_forward(*SEGMENTS[1], False)
            feed_forward(*SEGMENTS[2], True)
            for i in range(ADDED, B // 2):
                add_experts(i)

        @block.tensor
        def _(pe):
            pe.wait_ge(S["const_ready"], 9)
            for n in range(WARM):
                pe.matmul(ps_s[:, 0:128], ones[:, :], ones[:, :], start=True, stop=True)

            def turn_x(b):
                wait(pe, "xn_ready", b + 1)
                wait(pe, "q_lo_ready", b)
                wait(pe, "route_step", 3 * (b - 3) + 1)
                for t in range(T):
                    last = pe.transpose(ps_q[:, t * 128:(t + 1) * 128], xn[:, t, :], ident[:, :])
                last.then_inc(S["xt_done"], 1)

            def query(b):
                wait(pe, "xt_ready", b + 1)
                pe.matmul(ps_q[:, T * 128:], m_qk[:, :], xn_t[:, :], start=True, stop=True).then_inc(S["query_done"], 1)

            def scores(b, par, t, k):
                tile = T * b + t
                if t == 0 and k == 0:
                    wait(pe, "ctx_lo_ready", b + 1)
                    wait(pe, "q_lo_ready", b + 1)
                if k % 2 == 0:
                    wait(pe, "exp_done", 2 * (tile - 1) + k // 2 + 1)
                first = k // 2 * HALF + k % 2 * BANK
                cols = slice(first, min(first + BANK, (HALF, NKP)[k // 2]))
                qs = slice(t * 128, (t + 1) * 128)
                o = ps_s[:, k * BANK:k * BANK + cols.stop - cols.start]
                pe.matmul(o, q_hi[par][:, qs], ctx_hi[par][:, cols], start=True, stop=False)
                pe.matmul(o, q_hi[par][:, qs], ctx_lo[par][:, cols], start=False, stop=False)
                pe.matmul(o, q_lo[par][:, qs], ctx_hi[par][:, cols], start=False, stop=True).then_inc(S["scores_done"], 1)

            def turn_probs(b, t, g):
                tile = T * b + t
                if g < 2:
                    wait(pe, "exp_done", 2 * tile + g + 1)
                wait(pe, "pt_act" if g % 2 == 0 else "pt_dve", 2 * tile + g // 2)
                for c in range(4 * g, min(4 * g + 4, KC)):
                    n = min(128, NK - c * 128)
                    last = pe.transpose(ps_t[g % 2][0:n, (c % 4) * 128:(c % 4 + 1) * 128],
                                        probs[t][:, c * 128:c * 128 + n], ident[:, :])
                last.then_inc(S["turned_done"], 1)

            def weigh(b, half, par, chunks):
                tile = T * b + 1
                for c in chunks:
                    if c == 0:
                        wait(pe, ctx_n_in[par], 32 * half + 32)
                        wait(pe, "x2_ready", b)
                    if c % 4 == 0:
                        wait(pe, "pt_act" if c % 8 == 0 else "pt_dve", 2 * tile + c // 8 + 1)
                    n = min(128, NK - c * 128)
                    last = pe.matmul(ps_o[:, 0:T * 128], ctx_rows[par][0:n, c, :],
                                     probs_t[par][0:n, c, :, :].rearrange("p t q -> p (t q)"), start=(c == 0), stop=(c == KC - 1))
                if chunks[-1] == KC - 1:
                    last.then_inc(S["pv_done"], 1)

            def project(b):
                wait(pe, "o_ready", b + 1)
                for t in range(T):
                    last = pe.matmul(ps_o[:, (T + t) * 128:(T + t + 1) * 128], o_t[:, t * 128:(t + 1) * 128], w_vo[:, :],
                                     start=True, stop=True)
                last.then_inc(S["proj_done"], 1)

            def flat(v):
                return v.rearrange("p t e -> p (t e)")

            def places(b, par):
                wait(pe, "seen_ready", b + 1)
                pe.matmul(flat(ps_place), ones[:, :], flat(seen[:, :, :]), start=True, stop=False)
                pe.matmul(flat(ps_place), before[:, :], flat(onehot[:, par, :, :]), start=False, stop=True).then_inc(S["places_done"], 1)

            def turn_xn2(b, par):
                wait(pe, "xn2_ready", b + 1)
                for t in range(T):
                    last = pe.transpose(ps_q[:, t * 128:(t + 1) * 128], xn2[par][:, t, :], ident[:, :])
                last.then_inc(S["xn2_turned"], 1)

            def logits(b):
                wait(pe, "xn2_new_ready", b + 1)
                wait(pe, "xn2_hi_ready", b + 1)
                wait(pe, "place_step", 3 * (b - 1) + 1)
                for t in range(T):
                    last = pe.matmul(ps_logit[:, t, :], xn2_new[:, t * 128:(t + 1) * 128], w_router, start=True, stop=True)
                last.then_inc(S["logits_done"], 1)

            def step(b, half, par, has):
                earlier = half + (par - 1) // 2
                for k in range(SB):
                    if has(0):
                        scores(b, par, 0, k)
                    if k == 0 and has(-2):
                        project(b - 2)
                    if k < 3 and has(-1):
                        turn_probs(b - 1, 1, k)
                if starting(b):
                    turn_x(1)
                    query(1)
                if has(-1):
                    weigh(b - 1, earlier, 1 - par, range(0, 4))
                    turn_probs(b - 1, 1, 3)
                    weigh(b - 1, earlier, 1 - par, range(4, 6))
                if has(-3):
                    places(b - 3, 1 - par)
                if has(-2):
                    turn_xn2(b - 2, par)
                for k in range(SB):
                    if has(0):
                        scores(b, par, 1, k)
                        turn_probs(b, 0, k)
                    if k == 1 and has(-2):
                        logits(b - 2)
                if has(1) and not starting(b):
                    turn_x(b + 1)
                if has(-1):
                    weigh(b - 1, earlier, 1 - par, range(6, 9))
                if has(1) and not starting(b):
                    query(b + 1)
                if has(-1):
                    weigh(b - 1, earlier, 1 - par, range(9, KC))

            pe.wait_ge(S["matrix_ready"], 3)
            turn_x(0)
            pe.wait_ge(S["ld_w"], 16 * 2)
            pe.wait_ge(S["bias_cols"], 1)
            pe.matmul(ps_o[:, 0:128], w_q, w_k, start=True, stop=True)
            pe.matmul(ps_o[:, 384:385], w_k, b_q, start=True, stop=True)
            pe.matmul(ps_o[:, 128:256], w_v, w_o, start=True, stop=True)
            pe.matmul(ps_o[:, 256:384], b_v_cols[:, :], w_o, start=True, stop=True).then_inc(S["fold_done"], 1)
            pe.wait_ge(S["fold_ready"], 2)
            query(0)
            over_batches(pe, step, 1)

            def finish(m):
                if m == 0:
                    project(B - 1)
                elif m == 1:
                    places(B - 2, 0)
                elif m == 4:
                    turn_xn2(B - 1, 1)
                elif m == 5:
                    logits(B - 1)
                elif m == 8:
                    places(B - 1, 1)
                    pe.matmul(ps_count, ones[:, :], seen[:, 1, :], start=True, stop=False)
                    pe.matmul(ps_count, ones[:, :], onehot[:, 1, 1, :], start=False, stop=True).then_inc(S["counted"], 1)

            pe.wait_ge(S["ld_ffn"], 16)
            pe.wait_ge(S["w_lo_ready"], 2 + E)

            def turn_sorted(m, k, group):
                wait(pe, x_sorted_in[k], 16 * group + 16)
                wait(pe, "x_lo_ready", m - 1)
                pe.transpose(ps_x[k % 2][:, 0:128], x_sorted[k][:, 0:D], ident[:, :]).then_inc(S["xs_turned"], 1)

            expert_of = {n: pe.alloc_register(f"expert_of{n}") for n in range(-2, DEPTH)}
            for n in range(DEPTH):
                pe.reg_mov(expert_of[n], 0)

            for base, count, tile0, experts in SEGMENTS:
                snapped = {}

                def weights(k):
                    if not experts:
                        return E
                    if k in snapped:
                        return snapped[k]
                    return pe.snap(expert_of[k], min_val=0, max_val=E - 1)

                def item(m, group, k, has):
                    j = k % 2
                    if k == 0:
                        snapped.clear()
                    if has(0):
                        e = snapped[k] = weights(k)
                        if experts:
                            wait(pe, "x_lo_ready", m + 1)
                        wait(pe, "hid_ready", base + m - 1)
                        if experts:
                            settle(pe)
                            hi, lo = x_hi[j][:, :], x_lo[j][:, :]
                        else:
                            hi, lo = (part[:, bass.ds(tile0 + m, 1), :].rearrange("p o q -> p (o q)") for part in (xn2_hi, xn2_lo))
                        cols = bass.ds(e * 2 * FF, 2 * FF)
                        pe.matmul(ps_gu[j], hi, w_gu_hi[:, cols], start=True, stop=False)
                        pe.matmul(ps_gu[j], hi, w_gu_lo[:, cols], start=False, stop=False)
                        pe.matmul(ps_gu[j], lo, w_gu_hi[:, cols], start=False, stop=True).then_inc(S["gu_done"], 1)
                    if experts and k == DEPTH - 1:
                        for n in (-2, -1):
                            pe.reg_mov(expert_of[n], expert_of[n + DEPTH])
                        if has(1):
                            pe.load([expert_of[n] for n in range(DEPTH)], slot_weight_i[0:1, bass.ds(m + 1, DEPTH)])
                    if has(-1):
                        wait(pe, "hid_ready", base + m)
                        for c in range(FC):
                            last = pe.transpose(ps_ht[1 - j][:, c * 128:(c + 1) * 128], hid[1 - j][:, c * 128:(c + 1) * 128], ident[:, :])
                        last.then_inc(S["hid_turned"], 1)
                    if experts and has(2):
                        turn_sorted(m + 2, (k + 2) % DEPTH, group + (k + 2) // DEPTH)
                    if has(-2):
                        e = weights(k - 2)
                        wait(pe, "hid_t_ready", base + m - 1)
                        wait(pe, "y_kept", base + m - 3 if type(m) is not int or m > 2 else base)
                        if experts:
                            settle(pe)
                        for c in range(FC):
                            weight = w_down[:, bass.ds((e * FC + c) * D, D)] if experts else w_down_shared[:, c * D:(c + 1) * D]
                            last = pe.matmul(ps_y[j][:, 0:D], hid_t[j][:, c, :], weight,
                                             start=(c == 0), stop=(c == FC - 1))
                        last.then_inc(S["down_done"], 1)
                    if base == 0 and type(m) is int:
                        finish(m)

                pe.wait_ge(S["xn2_lo_ready"], B - 1 if base == 0 else B)
                if experts:
                    pe.wait_ge(S["w_down_in"], 16)
                    pe.wait_ge(S["table_ready"], 3)
                    pe.load([expert_of[n] for n in range(DEPTH)], slot_weight_i[0:1, 0:DEPTH])
                    for m in range(2):
                        turn_sorted(m, m, 0)
                over_items(pe, base, count, item)


def kernel(**inputs):
    import numpy as np
    import concourse.bacc as bacc
    from concourse.bass_utils import run_bass_kernel_spmd as run

    g = {k: np.asarray(v) for k, v in inputs.items()}
    ctx = g["ctx_1024"]
    B, NK, D = ctx.shape
    full = NK // 128 * 128
    arrays = {
        "x": g["x"],
        "ctx_t": ctx.transpose(0, 2, 1),
        "ctx_n": ctx[:, :full].reshape(B, full // 128, 128, D).transpose(0, 2, 1, 3),
        "ctx_tail": ctx[:, full:],
        "weights": np.concatenate([g["L0_xattn_Wq"], g["L0_xattn_Wk"], g["L0_xattn_Wv"], g["L0_xattn_Wo"].T,
                                   g["L0_ffn_router_w"].T, g["L0_xattn_bq"][:, None], g["L0_xattn_bv"][:, None]], axis=1),
        "bias_row": np.concatenate([g["L0_xattn_bo"], g["g_xattn"], g["g_ffn"]]),
        "expert_gu": np.concatenate([g["L0_ffn_expert_gate"], g["L0_ffn_expert_up"]], axis=2).transpose(1, 0, 2),
        "expert_down": g["L0_ffn_expert_down"],
        "shared_gu": np.concatenate([g["L0_ffn_shared_gate"], g["L0_ffn_shared_up"]], axis=1),
        "shared_down": g["L0_ffn_shared_down"],
    }
    arrays = {k: np.ascontiguousarray(v) for k, v in arrays.items()}
    nc = bacc.Bacc("TRN2", target_bir_lowering=False, num_devices=1)
    args = [nc.dram_tensor(k, v.shape, mybir.dt.from_np(v.dtype), kind="ExternalInput").ap() for k, v in arrays.items()]
    out = nc.dram_tensor("out", g["x"].shape, F32, kind="ExternalOutput").ap()
    flamingo_layer(nc, *args, out)
    return run(nc, [arrays], core_ids=[0]).results[0]["out"]
```
